# Optimizing a Trainium2 kernel written in Bass

```python
import numpy as np
import jax
import jax.numpy as jnp

def _softmax(x, axis=-1):
    return jax.nn.softmax(x, axis=axis)

def _gelu(x):
    return jax.nn.gelu(x, approximate=True)

def _silu(x):
    return jax.nn.silu(x)

def _sigmoid(x):
    return jax.nn.sigmoid(x)

def _layernorm(x, axis=-1, eps=1e-05):
    m = jnp.mean(x, axis=axis, keepdims=True)
    v = jnp.var(x, axis=axis, keepdims=True)
    return (x - m) / jnp.sqrt(v + eps)

def _scatter_add(tgt, idx, src, axis=0):
    return tgt.at[idx].add(src)

def _segment_sum(src, seg, n):
    return jax.ops.segment_sum(src, seg, n)
kernel_name = 'mk_adaln_attn_ffn_d1_seqx_r8_23c13e'

def setup_inputs(seed: int=0):
    np.random.seed(seed)
    _w = jnp.asarray

    def _rec_inputs():
        import jax
        import jax.numpy as jnp
        _rk = jax.random.key(seed)
        x = 7.22e-05 + 1 * jax.random.normal(jax.random.fold_in(_rk, 1), (32, 32, 256), jnp.float32)
        _lenS = 32 - jax.random.randint(jax.random.fold_in(_rk, 7), (32,), 0, max(1, 32 // 4) + 1, jnp.int32)
        _lenS2 = 32 - jax.random.randint(jax.random.fold_in(_rk, 8), (32,), 0, max(1, 32 // 4) + 1, jnp.int32)
        cond_2048 = 0.0061147 + 1.02565 * jax.random.normal(jax.random.fold_in(_rk, 11), (32, 256), jnp.float32)
        return (x, cond_2048)
    x, cond_2048 = _rec_inputs()

    def _L0_cond_setup():
        import jax, jax.numpy as jnp
        import numpy as np
        DIM = 256
        H = 16
        DH = 128
        INNER = H * DH
        MLP = 4 * DIM
        B, T = (2, 256)
        EPS = 1e-06

        def _ln(x):
            mu = jnp.mean(x, axis=-1, keepdims=True)
            var = jnp.var(x, axis=-1, keepdims=True)
            return (x - mu) * jax.lax.rsqrt(var + EPS)
        key = jax.random.key(seed)
        ks = jax.random.split(key, 12)
        s = 0.02
        return {'x': jax.random.normal(ks[0], (B, T, DIM), jnp.float32), 'timestep_embed': jax.random.normal(ks[1], (B, DIM), jnp.float32), 'ada_w': jax.random.normal(ks[2], (DIM, 6 * DIM), jnp.float32) * s, 'ada_b': jnp.zeros((6 * DIM,), jnp.float32), 'qkv_w': jax.random.normal(ks[3], (DIM, 3 * INNER), jnp.float32) * s, 'qkv_b': jnp.zeros((3 * INNER,), jnp.float32), 'out_w': jax.random.normal(ks[4], (INNER, DIM), jnp.float32) * s, 'out_b': jnp.zeros((DIM,), jnp.float32), 'ffn_w1': jax.random.normal(ks[5], (DIM, MLP), jnp.float32) * s, 'ffn_b1': jnp.zeros((MLP,), jnp.float32), 'ffn_w2': jax.random.normal(ks[6], (MLP, DIM), jnp.float32) * s, 'ffn_b2': jnp.zeros((DIM,), jnp.float32)}
    _L0_cond_all = _L0_cond_setup()
    _L0_cond_in = {k: v for k, v in _L0_cond_all.items() if k in ('ada_w', 'ada_b', 'qkv_w', 'qkv_b', 'out_w', 'out_b', 'ffn_w1', 'ffn_b1', 'ffn_w2', 'ffn_b2')}
    del _L0_cond_all

    def _L0_attn_setup():
        import jax, jax.numpy as jnp
        import numpy as np
        D = 256
        B, L = (4, 512)

        def log_g(x):
            return jnp.where(x >= 0, jnp.log(jax.nn.relu(x) + 0.5), -jax.nn.softplus(-x))
        key = jax.random.key(seed)
        kx, kz, kn = jax.random.split(key, 3)
        x = jax.random.normal(kx, (B, L, D), dtype=jnp.float32)
        std = np.sqrt(2.0 / D).astype(np.float32)
        Wz = jax.random.normal(kz, (D, D), dtype=jnp.float32) * std
        Wn = jax.random.normal(kn, (D, D), dtype=jnp.float32) * std
        bz = jnp.zeros((D,), dtype=jnp.float32)
        bn = jnp.zeros((D,), dtype=jnp.float32)
        return {'x': x, 'Wz': Wz, 'bz': bz, 'Wn': Wn, 'bn': bn}
    _L0_attn_all = _L0_attn_setup()
    _L0_attn_in = {k: v for k, v in _L0_attn_all.items() if k in ('Wz', 'bz', 'Wn', 'bn')}
    del _L0_attn_all

    def _L0_cond2_setup():
        import jax, jax.numpy as jnp
        import numpy as np
        DT = 0.01
        EPSILON = 0.08
        ALPHA = 0.7
        BETA = 0.8
        CLAMP = 20.0
        B, T, N = (32, 128, 256)

        def _derivative(q, p, drive, coupling, bias):
            i_couple = jnp.tanh(q) @ coupling.T
            dq = q - q ** 3 / 3.0 - p + drive + i_couple + bias
            dp = EPSILON * (q + ALPHA - BETA * p)
            return (dq, dp)

        def _rk4_step(q, p, drive, coupling, bias):
            dq1, dp1 = _derivative(q, p, drive, coupling, bias)
            dq2, dp2 = _derivative(q + 0.5 * DT * dq1, p + 0.5 * DT * dp1, drive, coupling, bias)
            dq3, dp3 = _derivative(q + 0.5 * DT * dq2, p + 0.5 * DT * dp2, drive, coupling, bias)
            dq4, dp4 = _derivative(q + DT * dq3, p + DT * dp3, drive, coupling, bias)
            q_next = q + DT / 6.0 * (dq1 + 2 * dq2 + 2 * dq3 + dq4)
            p_next = p + DT / 6.0 * (dp1 + 2 * dp2 + 2 * dp3 + dp4)
            q_next = jnp.clip(q_next, -CLAMP, CLAMP)
            p_next = jnp.clip(p_next, -CLAMP, CLAMP)
            return (q_next, p_next)
        key = jax.random.key(seed)
        k1, k2, k3, k4 = jax.random.split(key, 4)
        return {'q0': jax.random.normal(k1, (B, N), dtype=jnp.float32), 'p0': jax.random.normal(k2, (B, N), dtype=jnp.float32), 'input_drive_seq': jax.random.normal(k3, (B, T, N), dtype=jnp.float32), 'coupling': jax.random.normal(k4, (N, N), dtype=jnp.float32) * 0.01, 'bias': jnp.zeros((N,), dtype=jnp.float32)}
    _L0_cond2_all = _L0_cond2_setup()
    _L0_cond2_in = {k: v for k, v in _L0_cond2_all.items() if k in ('coupling', 'bias')}
    del _L0_cond2_all

    def _L0_ffn_setup():
        import jax, jax.numpy as jnp
        import numpy as np
        N_BLOCKS = 16
        BLOCK_SIZE = 64
        TOP_K = N_BLOCKS // 4
        key = jax.random.key(seed)
        k1, k2, k3, k4, k5 = jax.random.split(key, 5)
        in_f, out_f = (256, 1024)
        x = jax.random.normal(k1, (2, 512, in_f), dtype=jnp.float32)
        Wr = jax.random.normal(k2, (N_BLOCKS, in_f), dtype=jnp.float32) * in_f ** (-0.5)
        br = jnp.zeros((N_BLOCKS,), dtype=jnp.float32)
        W1 = jax.random.normal(k3, (out_f, in_f), dtype=jnp.float32) * in_f ** (-0.5)
        W2 = jax.random.normal(k4, (in_f, out_f), dtype=jnp.float32) * out_f ** (-0.5)
        return {'x': x, 'Wr': Wr, 'br': br, 'W1': W1, 'W2': W2}
    _L0_ffn_all = _L0_ffn_setup()
    _L0_ffn_in = {k: v for k, v in _L0_ffn_all.items() if k in ('Wr', 'br', 'W1', 'W2')}
    del _L0_ffn_all
    return {'x': x, 'cond_2048': cond_2048, 'L0_cond_ada_w': _L0_cond_in['ada_w'], 'L0_cond_ada_b': _L0_cond_in['ada_b'], 'L0_cond_qkv_w': _L0_cond_in['qkv_w'], 'L0_cond_qkv_b': _L0_cond_in['qkv_b'], 'L0_cond_out_w': _L0_cond_in['out_w'], 'L0_cond_out_b': _L0_cond_in['out_b'], 'L0_cond_ffn_w1': _L0_cond_in['ffn_w1'], 'L0_cond_ffn_b1': _L0_cond_in['ffn_b1'], 'L0_cond_ffn_w2': _L0_cond_in['ffn_w2'], 'L0_cond_ffn_b2': _L0_cond_in['ffn_b2'], 'L0_attn_Wz': _L0_attn_in['Wz'], 'L0_attn_bz': _L0_attn_in['bz'], 'L0_attn_Wn': _L0_attn_in['Wn'], 'L0_attn_bn': _L0_attn_in['bn'], 'L0_cond2_coupling': _L0_cond2_in['coupling'], 'L0_cond2_bias': _L0_cond2_in['bias'], 'L0_ffn_Wr': _L0_ffn_in['Wr'], 'L0_ffn_br': _L0_ffn_in['br'], 'L0_ffn_W1': _L0_ffn_in['W1'], 'L0_ffn_W2': _L0_ffn_in['W2']}

def reference(x, cond_2048, L0_cond_ada_w, L0_cond_ada_b, L0_cond_qkv_w, L0_cond_qkv_b, L0_cond_out_w, L0_cond_out_b, L0_cond_ffn_w1, L0_cond_ffn_b1, L0_cond_ffn_w2, L0_cond_ffn_b2, L0_attn_Wz, L0_attn_bz, L0_attn_Wn, L0_attn_bn, L0_cond2_coupling, L0_cond2_bias, L0_ffn_Wr, L0_ffn_br, L0_ffn_W1, L0_ffn_W2):
    import jax
    import jax.numpy as jnp

    def _L0_cond_ref(x, timestep_embed, ada_w, ada_b, qkv_w, qkv_b, out_w, out_b, ffn_w1, ffn_b1, ffn_w2, ffn_b2):
        import jax, jax.numpy as jnp
        import numpy as np
        DIM = 256
        H = 16
        DH = 128
        INNER = H * DH
        MLP = 4 * DIM
        B, T = (2, 256)
        EPS = 1e-06

        def _ln(x):
            mu = jnp.mean(x, axis=-1, keepdims=True)
            var = jnp.var(x, axis=-1, keepdims=True)
            return (x - mu) * jax.lax.rsqrt(var + EPS)
        Bc, Tc, D = x.shape
        ada = (timestep_embed @ ada_w + ada_b)[:, None, :]
        shift1, scale1, gate1, shift2, scale2, gate2 = jnp.split(ada, 6, axis=-1)
        x1 = _ln(x) * (1.0 + scale1) + shift1
        qkv = (x1 @ qkv_w + qkv_b).reshape(Bc, Tc, 3, H, DH)
        q, k, v = (qkv[:, :, 0], qkv[:, :, 1], qkv[:, :, 2])
        scale = DH ** (-0.5)
        attn = jnp.einsum('bthd,bshd->bhts', q, k) * scale
        attn = jax.nn.softmax(attn, axis=-1)
        attn_out = jnp.einsum('bhts,bshd->bthd', attn, v).reshape(Bc, Tc, INNER)
        attn_out = attn_out @ out_w + out_b
        x = x + gate1 * attn_out
        x2 = _ln(x) * (1.0 + scale2) + shift2
        h = jax.nn.gelu(x2 @ ffn_w1 + ffn_b1, approximate=False)
        x = x + gate2 * (h @ ffn_w2 + ffn_b2)
        return x

    def _L0_attn_ref(x, Wz, bz, Wn, bn):
        import jax, jax.numpy as jnp
        import numpy as np
        D = 256
        B, L = (4, 512)

        def log_g(x):
            return jnp.where(x >= 0, jnp.log(jax.nn.relu(x) + 0.5), -jax.nn.softplus(-x))
        Bq, Lq, Dq = x.shape
        k = jnp.einsum('bld,ed->ble', x, Wz) + bz
        log_z = -jax.nn.softplus(-k)
        log_coeffs = -jax.nn.softplus(k)
        log_h0 = jnp.full((Bq, 1, Dq), jnp.log(0.5), dtype=x.dtype)
        log_h_ = log_g(jnp.einsum('bld,ed->ble', x, Wn) + bn)
        log_values = jnp.concatenate([log_h0, log_z + log_h_], axis=1)
        a_star = jnp.pad(jnp.cumsum(log_coeffs, axis=1), ((0, 0), (1, 0), (0, 0)))
        log_h = a_star + jax.lax.cumlogsumexp(log_values - a_star, axis=1)
        return jnp.exp(log_h)[:, 1:]

    def _L0_cond2_ref(q0, p0, input_drive_seq, coupling, bias):
        import jax, jax.numpy as jnp
        import numpy as np
        DT = 0.01
        EPSILON = 0.08
        ALPHA = 0.7
        BETA = 0.8
        CLAMP = 20.0
        B, T, N = (32, 128, 256)

        def _derivative(q, p, drive, coupling, bias):
            i_couple = jnp.tanh(q) @ coupling.T
            dq = q - q ** 3 / 3.0 - p + drive + i_couple + bias
            dp = EPSILON * (q + ALPHA - BETA * p)
            return (dq, dp)

        def _rk4_step(q, p, drive, coupling, bias):
            dq1, dp1 = _derivative(q, p, drive, coupling, bias)
            dq2, dp2 = _derivative(q + 0.5 * DT * dq1, p + 0.5 * DT * dp1, drive, coupling, bias)
            dq3, dp3 = _derivative(q + 0.5 * DT * dq2, p + 0.5 * DT * dp2, drive, coupling, bias)
            dq4, dp4 = _derivative(q + DT * dq3, p + DT * dp3, drive, coupling, bias)
            q_next = q + DT / 6.0 * (dq1 + 2 * dq2 + 2 * dq3 + dq4)
            p_next = p + DT / 6.0 * (dp1 + 2 * dp2 + 2 * dp3 + dp4)
            q_next = jnp.clip(q_next, -CLAMP, CLAMP)
            p_next = jnp.clip(p_next, -CLAMP, CLAMP)
            return (q_next, p_next)
        drive_tbn = jnp.swapaxes(input_drive_seq, 0, 1)

        def scan_fn(carry, drive):
            q, p = carry
            q, p = _rk4_step(q, p, drive, coupling, bias)
            return ((q, p), q)
        (_, _), q_trace_tbn = jax.lax.scan(scan_fn, (q0, p0), drive_tbn)
        return jnp.swapaxes(q_trace_tbn, 0, 1)

    def _L0_ffn_ref(x, Wr, br, W1, W2):
        import jax, jax.numpy as jnp
        import numpy as np
        N_BLOCKS = 16
        BLOCK_SIZE = 64
        TOP_K = N_BLOCKS // 4
        x_shape = x.shape
        in_f = x_shape[-1]
        xf = x.reshape(-1, in_f)
        n = xf.shape[0]
        prob = jax.nn.softmax(xf @ Wr.T + br, axis=-1)
        _, idx = jax.lax.top_k(prob, TOP_K)
        mask = jnp.zeros((n, N_BLOCKS), dtype=xf.dtype)
        mask = mask.at[jnp.arange(n)[:, None], idx].set(1.0)
        W1b = W1.reshape(N_BLOCKS, BLOCK_SIZE, in_f)
        h = jnp.einsum('nf,ibf->nib', xf, W1b)
        h = jax.nn.gelu(h, approximate=False) * mask[:, :, None]
        W2b = W2.reshape(in_f, N_BLOCKS, BLOCK_SIZE)
        y = jnp.einsum('nib,fib->nf', h, W2b)
        return y.reshape(x_shape)
    x = x + _L0_attn_ref(_L0_cond_ref(x, cond_2048, L0_cond_ada_w, L0_cond_ada_b, L0_cond_qkv_w, L0_cond_qkv_b, L0_cond_out_w, L0_cond_out_b, L0_cond_ffn_w1, L0_cond_ffn_b1, L0_cond_ffn_w2, L0_cond_ffn_b2), L0_attn_Wz, L0_attn_bz, L0_attn_Wn, L0_attn_bn)
    x = x + _L0_ffn_ref(_L0_cond2_ref(cond_2048, cond_2048, x, L0_cond2_coupling, L0_cond2_bias), L0_ffn_Wr, L0_ffn_br, L0_ffn_W1, L0_ffn_W2)
    return x

_drawn_inputs = setup_inputs


def setup_inputs(seed=0):
    import zlib

    import numpy as np

    out = dict(_drawn_inputs(seed))
    spreads = {'L0_cond_ada_b': (0.0, 0.412),
     'L0_cond_qkv_b': (0.0, 0.36),
     'L0_cond_out_b': (0.0, 0.299),
     'L0_cond_ffn_b1': (0.0, 0.8),
     'L0_cond_ffn_b2': (0.0, 0.297),
     'L0_attn_bz': (0.0, 0.509),
     'L0_attn_bn': (0.0, 0.1),
     'L0_cond2_bias': (0.0, 0.285),
     'L0_ffn_br': (0.0, 0.1)}
    factors = {}
    for name, (base, spread) in spreads.items():
        noise = np.random.default_rng([zlib.crc32(name.encode()), seed]).standard_normal(out[name].shape)
        drawn = base * np.exp(spread * noise) if base else spread * noise
        out[name] = jnp.asarray(drawn.astype(out[name].dtype))
    for name, factor in factors.items():
        out[name] = (out[name] * factor).astype(out[name].dtype)
    return out
```

```python
from contextlib import ExitStack

import concourse.bass as bass
from concourse import mybir

ALU = mybir.AluOpType
ACT = mybir.ActivationFunctionType
F32 = mybir.dt.float32
F16 = mybir.dt.float16
BF16 = mybir.dt.bfloat16
AX_X = mybir.AxisListType.X

P = 128
B, T, D = 32, 32, 256
N = B * T
KB = D // P
H, DH = 16, 128
QUAD = 4
NQUAD = H // QUAD
HALF = N // 2
NH = N // HALF
G = N // P
NB4 = P // T
MLP = 4 * D
MB = MLP // P
NBLK, TOPK = 16, 4
LN_EPS = 1e-6
SCALE = float(DH) ** -0.5
DT, EPSILON, ALPHA, BETA, CLAMP = 0.01, 0.08, 0.7, 0.8, 20.0
STAGE_H = (0.5 * DT, 0.5 * DT, DT, DT / 6.0)
BIG = 3.0e38

VEC = {}
_at = 0
for _name, _n in (("ada_b", 12), ("q_b", H), ("k_b", H), ("v_b", H), ("out_b", KB), ("ffn_b1", MB), ("ffn_b2", KB),
                  ("bz", KB), ("bn", KB), ("c2_b", KB)):
    VEC[_name] = (_at, _at + _n)
    _at += _n
NVEC = _at

SHIFT1, SCALE1, GATE1, SHIFT2, SCALE2, GATE2 = range(6)

USE_PROJ = [0, 12, 18, 24]
USE_V = 4
USE_PV = [16, 22, 28, 30]
USES_PER_PASS = 32


def build(nc, xT, condT, ada_w, vecs, br, wqk, wv, wo, ffn_w1, ffn_w2, wzT, wnT, coupT, wrT, w1T, w2T, out):
    with ExitStack() as ctx:
        def sb(name, shape, dt=F32):
            return ctx.enter_context(nc.sbuf_tensor(name, shape, dt))

        def sem(name):
            return ctx.enter_context(nc.semaphore(name))

        bank = [ctx.enter_context(nc.psum_tensor(f"bank{i}", [P, 512], F32)) for i in range(2)]
        score = ctx.enter_context(nc.psum_tensor("score", [P, 2, 512], F32))
        proj = ctx.enter_context(nc.psum_tensor("proj", [P, KB * NH, 512], F32))

        x_sb = sb("x_sb", [P, KB, N])
        cond_sb = sb("cond_sb", [P, KB, B])
        adaw_sb = sb("adaw_sb", [P, KB, 6 * D])
        vec = sb("vec", [P, NVEC])
        br_sb = sb("br_sb", [P, NBLK])
        wqk_sb = sb("wqk_sb", [P, QUAD, KB, 2, DH])
        wv_sb = sb("wv_sb", [P, KB, QUAD * DH])
        wo_sb = sb("wo_sb", [P, QUAD, D])
        f1_sb = sb("f1_sb", [P, KB, MLP])
        f2_sb = sb("f2_sb", [P, MB, D])
        wz_sb = sb("wz_sb", [P, KB, D])
        wn_sb = sb("wn_sb", [P, KB, D])
        coup_sb = sb("coup_sb", [P, KB, D])
        coup_rest = sb("coup_rest", [P, KB, D])
        coup_parts = [sb(f"coup_part{i}", [P, KB, D], BF16) for i in range(3)]
        wr_sb = sb("wr_sb", [P, KB, NBLK])
        w1_sb = sb("w1_sb", [P, KB, MLP])
        w2_sb = sb("w2_sb", [P, MB, D])

        ones = sb("ones", [P, P])
        ident = sb("ident", [P, P], BF16)

        ada = sb("ada", [P, 6, KB, B])
        centred = sb("centred", [P, KB, HALF])
        square = sb("square", [P, KB, HALF])
        var = sb("var", [P, HALF])
        std = sb("std", [P, HALF])
        rstd = sb("rstd", [P, HALF])
        x1 = sb("x1", [P, KB, N])

        big = sb("big", [P, 2 * 4096])
        qk_sb = big[:, 0:4096].rearrange("p (r w n) -> p r w n", r=2, w=2)
        v_sb = big[:, 4096:8192].rearrange("p (g n) -> p g n", g=G)
        hid = big[:, :].rearrange("p (m n) -> p m n", m=MB)
        ao_sb = sb("ao_sb", [P, QUAD, N])
        pass_b = sb("pass_b", [P, 3, QUAD])
        smax = sb("smax", [P, G])
        ssum = sb("ssum", [P, G])
        srec = sb("srec", [P, G])
        sc = sb("sc", [P, G, T])
        pe_ = sb("pe_", [P, G, T])
        pn = sb("pn", [P, G, T])
        pt = sb("pt", [P, G, T])
        unit = sb("unit", [P, G, T])
        ptx = sb("ptx", [P, G, P])
        acc = sb("acc", [P, KB, N])

        hb = sb("hb", [P, 2 * KB])
        tz = sb("tz", [P, HALF])
        nn_ = sb("nn_", [P, HALF])
        nneg = square[:, 0]
        tn = sb("tn", [P, HALF])
        npos = sb("npos", [P, HALF])
        za = sb("za", [P, HALF])
        zb = square[:, 1]
        drive = sb("drive", [P, KB, N])
        dbias = sb("dbias", [P, T, KB * B])

        qst = sb("qst", [P, 4, KB * B])
        pst = sb("pst", [P, 4, KB * B])
        trace = wqk_sb[:].rearrange("p j k w d -> p (j k w d)").rearrange("p (k t b) -> p k t b", k=KB, t=T)
        th16 = sb("th16", [P, KB * B], F16)
        th32 = sb("th32", [P, KB * B])
        thlo = sb("thlo", [P, KB * B], F16)
        sq = sb("sq", [P, KB * B])
        cub = sb("cub", [P, KB * B])
        base = sb("base", [P, KB * B])
        qd = sb("qd", [P, 2, KB * B])
        pc = sb("pc", [P, KB * B])
        pfac = sb("pfac", [P, 3, KB * B])
        bp = sb("bp", [P, KB * B])
        rp = sb("rp", [P, KB * B])
        qsum = sb("qsum", [P, KB * B])
        psum_ = sb("psum_", [P, KB * B])
        qn = sb("qn", [P, KB * B])

        lg = sb("lg", [P, G, NBLK + TOPK])
        top8 = sb("top8", [P, G, 8])
        lgr = sb("lgr", [P, G, NBLK + TOPK])
        mask = sb("mask", [P, G, NBLK], BF16)
        maskx = ao_sb[:].rearrange("p j n -> p (j n)").bitcast(BF16).rearrange("p (g n) -> p g n", g=G)
        osb = x1

        def v_(name, j=None):
            a, b = VEC[name]
            return vec[:, a:b] if j is None else vec[:, a + j:a + j + 1]

        x_loaded = sem("x_loaded")
        small_loaded = sem("small_loaded")
        late_loaded = sem("late_loaded")
        qk_loaded = [sem(f"qk_loaded{j}") for j in range(QUAD)]
        v_loaded = sem("v_loaded")
        o_loaded = sem("o_loaded")
        ones_ready = sem("ones_ready")
        ident_ready = sem("ident_ready")
        ada_summed = sem("ada_summed")
        ada_ready = sem("ada_ready")
        mean_ready = sem("mean_ready")
        var_ready = sem("var_ready")
        centred_ready = sem("centred_ready")
        square_ready = sem("square_ready")
        var_copied = sem("var_copied")
        rstd_ready = sem("rstd_ready")
        x1_ready = sem("x1_ready")
        dve_step = sem("dve_step")
        pool_step = sem("pool_step")
        act_step = sem("act_step")
        full = [sem(f"full{i}") for i in range(2)]
        free = [sem(f"free{i}") for i in range(2)]
        bias_ready = sem("bias_ready")
        scores_ready = sem("scores_ready")
        shifted = sem("shifted")
        exp_ready = sem("exp_ready")
        pt_ready = sem("pt_ready")
        ptx_ready = sem("ptx_ready")
        weights_used = [sem(f"weights_used{j}") for j in range(QUAD)]
        v_weights_used = sem("v_weights_used")
        proj_ready = sem("proj_ready")
        proj_added = sem("proj_added")
        coup_ready = sem("coup_ready")
        hid_ready = sem("hid_ready")
        x3_ready = sem("x3_ready")
        gate_in = sem("gate_in")
        gate_th = sem("gate_th")
        z_ready = sem("z_ready")
        z_used = sem("z_used")
        tn_ready = sem("tn_ready")
        drive_ready = sem("drive_ready")
        q_ready = sem("q_ready")
        th16_ready = sem("th16_ready")
        th32_ready = sem("th32_ready")
        lo_ready = sem("lo_ready")
        coupled = sem("coupled")
        p_ready = sem("p_ready")
        bp_ready = sem("bp_ready")
        logits_ready = sem("logits_ready")
        mask_ready = sem("mask_ready")
        maskb_ready = sem("maskb_ready")
        maskb_used = sem("maskb_used")
        gelu_ready = sem("gelu_ready")
        h_ready = sem("h_ready")
        out_ready = sem("out_ready")
        stored = sem("stored")

        AFTER = NQUAD * USES_PER_PASS
        USE_F1 = [AFTER, AFTER + MB + KB]
        USE_GRU = [AFTER + 2 * (MB + KB) + 2 * KB * h for h in range(NH)]
        USE_G1 = [AFTER + 2 * (MB + KB) + 2 * KB * NH + (MB + KB) * h for h in range(NH)]

        def bank_of(use):
            return use % 2

        def count_of(use, start=0):
            return start * (USES_PER_PASS // 2) + use // 2 + 1

        NPAR = USES_PER_PASS // 2

        class Own:

            def __init__(self, eng, semaphore):
                self.eng, self.sem, self.n, self.base = eng, semaphore, 0, 0

            def step(self, ins):
                ins.then_inc(self.sem, 1)
                self.n += 1

            def wait(self):
                self.eng.wait_ge(self.sem, self.base + self.n)

        block = ctx.enter_context(nc.Block())

        @block.sync
        def _(sp):
            sp.dma_start(x_sb[:, :, 0:HALF], xT[:, :, 0:HALF]).then_inc(x_loaded, 16)
            sp.dma_start(x_sb[:, :, HALF:N], xT[:, :, HALF:N]).then_inc(x_loaded, 16)
            for j in range(QUAD):
                sp.dma_start(wqk_sb[:, j], wqk[j]).then_inc(qk_loaded[j], 16)
            sp.dma_start(wv_sb[:], wv[0]).then_inc(v_loaded, 16)
            sp.dma_start(wo_sb[:], wo[:, 0:QUAD]).then_inc(o_loaded, 16)
            with sp.Fori(0, NQUAD - 1) as i:
                for j in range(QUAD):
                    sp.wait_ge(weights_used[j], i + 1)
                    sp.dma_start(wqk_sb[:, j], wqk[bass.ds(i * QUAD + QUAD + j, 1)].rearrange("a p k w d -> (a p) k w d")
                                 ).then_inc(qk_loaded[j], 16)
                    if j == 0:
                        sp.wait_ge(v_weights_used, i + 1)
                        sp.dma_start(wv_sb[:], wv[bass.ds(i + 1, 1)].rearrange("a p k n -> (a p) k n")
                                     ).then_inc(v_loaded, 16)
                sp.wait_ge(proj_ready, i + 1)
                sp.dma_start(wo_sb[:], wo[:, bass.ds(i * QUAD + QUAD, QUAD)]).then_inc(o_loaded, 16)
            for h in range(NH):
                for ob in range(KB):
                    sp.wait_ge(out_ready, h * KB + ob + 1)
                    sp.dma_start(out[:, ob, h * HALF:(h + 1) * HALF], osb[:, ob, h * HALF:(h + 1) * HALF]
                                 ).then_inc(stored, 16)
            sp.wait_ge(stored, 16 * KB * NH)

        @block.gpsimd
        def _(pool):
            own = Own(pool, pool_step)
            nc.gpsimd.memset(ones[:], 1.0 / D).then_inc(ones_ready, 1)
            own.step(nc.gpsimd.memset(ident[:], 0.0))
            own.wait()
            nc.gpsimd.affine_select(out=ident[:], in_=ident[:], compare_op=ALU.not_equal, fill=1.0, base=0,
                                    pattern=[[-1, P]], channel_multiplier=1).then_inc(ident_ready, 1)
            own.step(nc.gpsimd.memset(ptx[:], 0.0))
            own.step(nc.gpsimd.memset(unit[:], 1.0))
            for s in range(3):
                own.step(nc.gpsimd.memset(pfac[:, s], -BETA * STAGE_H[s] * EPSILON))

            own.wait()
            with pool.Fori(0, NQUAD) as i:
                for j in range(QUAD):
                    pool.wait_ge(pt_ready, i * QUAD + j + 1)
                    for q in range(NB4):
                        s = slice(q * T, (q + 1) * T)
                        nc.gpsimd.tensor_tensor(ptx[s, :, s], pt[s], unit[s], ALU.mult).then_inc(ptx_ready, 1)
            pool.wait_ge(ptx_ready, NQUAD * QUAD * NB4)
            start = own.n
            with pool.Fori(0, T) as t:
                own.n, own.base = 0, t * 5 + start
                for s in range(3):
                    pool.wait_ge(p_ready, t * 4 + s + 1)
                    own.step(nc.gpsimd.tensor_tensor(bp[:], pst[:, s], pfac[:, s], ALU.mult))
                    if s != 1:
                        own.step(nc.gpsimd.tensor_scalar(pc[:], pst[:, 0], STAGE_H[s] * EPSILON * ALPHA, None, ALU.add))
                    own.wait()
                    nc.gpsimd.tensor_tensor(bp[:], bp[:], pc[:], ALU.add).then_inc(bp_ready, 1)
                assert own.n == 5

        @block.scalar
        def _(act):
            own = Own(act, act_step)
            act.dma_start(cond_sb[:], condT).then_inc(small_loaded, 16)
            act.dma_start(adaw_sb[:], ada_w).then_inc(small_loaded, 16)
            act.dma_start(vec[:], vecs).then_inc(small_loaded, 16)
            for dst, src in ((br_sb, br), (f1_sb, ffn_w1), (f2_sb, ffn_w2), (wz_sb, wzT), (wn_sb, wnT),
                             (coup_sb, coupT), (wr_sb, wrT), (w1_sb, w1T), (w2_sb, w2T)):
                act.dma_start(dst[:], src).then_inc(late_loaded, 16)

            def squares(n):
                act.wait_ge(centred_ready, n + 1)
                nc.scalar.activation(square[:], centred[:], ACT.Square).then_inc(square_ready, 1)

            def roots(n):
                act.wait_ge(var_copied, n + 1)
                nc.scalar.activation(std[:], var[:], ACT.Sqrt).then_inc(rstd_ready, 1)

            squares(0)
            roots(0)
            squares(1)
            roots(1)

            with act.Fori(0, NQUAD) as i:
                def empty(use, dst, bias=None):
                    act.wait_ge(full[bank_of(use)], i * NPAR + count_of(use))
                    src = bank[bank_of(use)][:]
                    if bias is None:
                        ins = nc.scalar.activation(dst, src, ACT.Copy)
                    else:
                        ins = nc.scalar.activation(dst, src, ACT.Identity, bias=bias)
                    ins.then_inc(free[bank_of(use)], 1)

                def head_bias(name, j):
                    return pass_b[:, ("q_b", "k_b", "v_b").index(name), j:j + 1]

                act.wait_ge(bias_ready, i * 3 + 3)

                def empty_proj(j, k):
                    w, h = k // NH, k % NH
                    empty(USE_PROJ[j] + k, qk_sb[:, j % 2, w, h * HALF:(h + 1) * HALF],
                          head_bias(("q_b", "k_b")[w], j))

                def empty_pv(j):
                    for h in range(NH):
                        empty(USE_PV[j] + h, ao_sb[:, j, h * HALF:(h + 1) * HALF], head_bias("v_b", j))

                def exps(j):
                    act.wait_ge(shifted, i * (QUAD * NB4) + NB4 * (j + 1))
                    nc.scalar.activation(pe_[:], sc[:], ACT.Exp, scale=SCALE).then_inc(exp_ready, 1)

                for k in range(4):
                    empty_proj(0, k)
                for g in range(G):
                    empty(USE_V + g, v_sb[:, g])
                    if g == 2:
                        exps(0)
                for j in range(QUAD):
                    if j + 1 < QUAD:
                        for k in range(4):
                            empty_proj(j + 1, k)
                            if k == 1 and j >= 1:
                                exps(j)
                    else:
                        exps(j)
                    empty_pv(j)

            def empty(use, dst, func, bias=0.0, scale=1.0):
                act.wait_ge(full[bank_of(use)], count_of(use))
                nc.scalar.activation(dst, bank[bank_of(use)][:], func, bias=bias, scale=scale
                                     ).then_inc(free[bank_of(use)], 1)

            for h in range(NH):
                squares(NH + h)
                roots(NH + h)
            for h in range(NH):
                for m in range(MB):
                    if h == 0 and m == 0:
                        act.wait_ge(proj_ready, NQUAD)
                    empty(USE_F1[h] + m, hid[:, m, h * HALF:(h + 1) * HALF], ACT.Gelu, bias=v_("ffn_b1", m))
            act.wait_ge(coup_ready, 1)
            n = 0
            for h in range(NH):
                for ob in range(KB):
                    use = USE_GRU[h] + 2 * ob
                    if n:
                        act.wait_ge(z_used, n)
                    empty(use, tz[:], ACT.Tanh, bias=hb[:, ob:ob + 1], scale=0.5)
                    empty(use + 1, nn_[:], ACT.Identity, bias=v_("bn", ob))
                    act.wait_ge(gate_in, n + 1)
                    nc.scalar.activation(tn[:], nneg, ACT.Tanh, scale=0.5).then_inc(tn_ready, 1)
                    n += 1

            with act.Fori(0, T) as t:
                for s in range(4):
                    act.wait_ge(q_ready, t * 4 + s + 1)
                    nc.scalar.activation(th16[:], qst[:, s], ACT.Tanh).then_inc(th16_ready, 1)
                    nc.scalar.activation(th32[:], qst[:, s], ACT.Tanh).then_inc(th32_ready, 1)

            for h in range(NH):
                for m in range(MB):
                    empty(USE_G1[h] + m, hid[:, m, h * HALF:(h + 1) * HALF], ACT.Gelu)

        @block.tensor
        def _(pe):
            def mm(dst, lhsT, rhs, start, stop, **kw):
                return nc.tensor.matmul(dst, lhsT, rhs, start=start, stop=stop, **kw)

            pe.wait_ge(small_loaded, 48)
            pe.wait_ge(ones_ready, 1)
            for c in range(6 * KB):
                for k in range(KB):
                    last = mm(score[:, 0, c * B:(c + 1) * B], adaw_sb[:, k, c * P:(c + 1) * P], cond_sb[:, k],
                              k == 0, k == KB - 1)
            last.then_inc(ada_summed, 1)

            def mean_of(src, n):
                h = n % NH
                for k in range(KB):
                    last = mm(proj[:, h], ones[:], src[:, k, h * HALF:(h + 1) * HALF], k == 0, k == KB - 1)
                last.then_inc(mean_ready, 1)

            def var_of(n):
                pe.wait_ge(square_ready, n + 1)
                for k in range(KB):
                    last = mm(proj[:, NH + n % NH], ones[:], square[:, k], k == 0, k == KB - 1)
                last.then_inc(var_ready, 1)

            pe.wait_ge(x_loaded, 32)
            for h in range(NH):
                mean_of(x_sb, h)
            for h in range(NH):
                var_of(h)
            pe.wait_ge(x1_ready, NH)

            with pe.Fori(0, NQUAD) as i:
                def fill(use):
                    pe.wait_ge(free[bank_of(use)], i * NPAR + count_of(use))
                    return bank[bank_of(use)]

                def taken(use):
                    pe.wait_ge(free[bank_of(use)], i * NPAR + count_of(use) + 1)

                def project(j):
                    pe.wait_ge(qk_loaded[j], i * 16 + 16)
                    for w in range(2):
                        for h in range(NH):
                            use = USE_PROJ[j] + w * NH + h
                            dst = fill(use)
                            for k in range(KB):
                                last = mm(dst[:], wqk_sb[:, j, k, w], x1[:, k, h * HALF:(h + 1) * HALF],
                                          k == 0, k == KB - 1)
                                if j == 1 and w == 0 and h == 0 and k == 0:
                                    last.then_inc(v_weights_used, 1)
                            last.then_inc(full[bank_of(use)], 1)

                def scores(j):
                    taken(USE_PROJ[j] + 2)
                    taken(USE_PROJ[j] + 3)
                    for g in range(G):
                        last = mm(score[:, g // 4, (g % 4) * P:(g % 4 + 1) * P], qk_sb[:, j % 2, 0, g * P:(g + 1) * P],
                                  qk_sb[:, j % 2, 1, g * P:(g + 1) * P], True, True)
                        if g == 0:
                            last.then_inc(weights_used[j], 1)
                    last.then_inc(scores_ready, 1)

                def values():
                    pe.wait_ge(v_loaded, i * 16 + 16)
                    for g in range(G):
                        use = USE_V + g
                        dst = fill(use)
                        for k in range(KB):
                            last = mm(dst[:], x1[:, k, g * P:(g + 1) * P], wv_sb[:, k], k == 0, k == KB - 1)
                        last.then_inc(full[bank_of(use)], 1)

                def mix(j):
                    if j == 0:
                        taken(USE_V + G - 2)
                        taken(USE_V + G - 1)
                    pe.wait_ge(ptx_ready, i * (QUAD * NB4) + NB4 * (j + 1))
                    for h in range(NH):
                        use = USE_PV[j] + h
                        dst = fill(use)
                        for g in range(4 * h, 4 * h + 4):
                            last = mm(dst[:, (g % 4) * P:(g % 4 + 1) * P], v_sb[:, g, j * DH:(j + 1) * DH],
                                      ptx[:, g], True, True)
                        last.then_inc(full[bank_of(use)], 1)

                def out_project(j):
                    taken(USE_PV[j])
                    taken(USE_PV[j] + 1)
                    if j == 0:
                        pe.wait_ge(o_loaded, i * 16 + 16)
                        pe.wait_ge(proj_added, i * (KB * NH) + KB * NH)
                    for ob in range(KB):
                        for h in range(NH):
                            last = mm(proj[:, ob * NH + h], wo_sb[:, j, ob * P:(ob + 1) * P],
                                      ao_sb[:, j, h * HALF:(h + 1) * HALF], j == 0, j == QUAD - 1,
                                      skip_group_check=True)
                    if j == QUAD - 1:
                        last.then_inc(proj_ready, 1)

                project(0)
                scores(0)
                values()
                for j in range(QUAD):
                    if j + 1 < QUAD:
                        project(j + 1)
                    mix(j)
                    if j + 1 < QUAD:
                        scores(j + 1)
                    if j == 1:
                        out_project(0)
                    if j == 2:
                        out_project(1)
                        out_project(2)
                out_project(QUAD - 1)

            def fill(use):
                pe.wait_ge(free[bank_of(use)], count_of(use))
                return bank[bank_of(use)]

            def product(use, weights, rhs, nk):
                dst = fill(use)
                for k in range(nk):
                    last = mm(dst[:], weights(k), rhs(k), k == 0, k == nk - 1)
                last.then_inc(full[bank_of(use)], 1)

            pe.wait_ge(proj_added, KB * NH * (NQUAD + 1) + 1)
            for h in range(NH):
                mean_of(acc, NH + h)
            for h in range(NH):
                var_of(NH + h)
            pe.wait_ge(late_loaded, 9 * 16)
            for h in range(NH):
                s = slice(h * HALF, (h + 1) * HALF)
                pe.wait_ge(x1_ready, NH + h + 1)
                for m in range(MB):
                    product(USE_F1[h] + m, lambda k: f1_sb[:, k, m * P:(m + 1) * P], lambda k: x1[:, k, s], KB)
                for b in range(2):
                    pe.wait_ge(free[b], count_of(USE_F1[h] + MB - 2 + b) + 1)
                for ob in range(KB):
                    product(USE_F1[h] + MB + ob, lambda k: f2_sb[:, k, ob * P:(ob + 1) * P], lambda k: hid[:, k, s], MB)
            for h in range(NH):
                s = slice(h * HALF, (h + 1) * HALF)
                pe.wait_ge(x3_ready, (h + 1) * KB)
                for ob in range(KB):
                    for w, weights in enumerate((wz_sb, wn_sb)):
                        product(USE_GRU[h] + 2 * ob + w, lambda k: weights[:, k, ob * P:(ob + 1) * P],
                                lambda k: acc[:, k, s], KB)

            with pe.Fori(0, T) as t:
                for s in range(4):
                    dst = score[:, 0]
                    pe.wait_ge(th16_ready, t * 4 + s + 1)
                    first = True
                    for parts, src, ready in ((coup_parts, th16, None), (coup_parts[0:2], thlo, lo_ready)):
                        if ready is not None:
                            pe.wait_ge(ready, t * 4 + s + 1)
                        for part in parts:
                            for ob in range(KB):
                                for k in range(KB):
                                    last = mm(dst[:, ob * B:(ob + 1) * B], part[:, k, ob * P:(ob + 1) * P],
                                              src[:, k * B:(k + 1) * B], first, False, skip_group_check=True)
                                    first = False
                    last.then_inc(coupled, 1)

            flat = trace.rearrange("p k t b -> p k (t b)")
            pe.wait_ge(q_ready, 4 * T + 1)
            for g in range(G):
                for k in range(KB):
                    last = mm(score[:, 1, g * NBLK:(g + 1) * NBLK], flat[:, k, g * P:(g + 1) * P], wr_sb[:, k],
                              k == 0, k == KB - 1)
            last.then_inc(logits_ready, 1)
            n = 0
            for h in range(NH):
                s = slice(h * HALF, (h + 1) * HALF)
                for m in range(MB):
                    product(USE_G1[h] + m, lambda k: w1_sb[:, k, m * P:(m + 1) * P], lambda k: flat[:, k, s], KB)
                    if h == 0 and m == 0:
                        pe.wait_ge(mask_ready, G)
                    if n >= 4:
                        pe.wait_ge(maskb_used, n - 3)
                    for g in range(4):
                        last = mm(proj[:, n % 4, g * P:(g + 1) * P], maskx[:, 4 * h + g, m * P:(m + 1) * P],
                                  ident[:], True, True)
                    last.then_inc(maskb_ready, 1)
                    n += 1
                pe.wait_ge(h_ready, (h + 1) * MB)
                for ob in range(KB):
                    product(USE_G1[h] + MB + ob, lambda k: w2_sb[:, k, ob * P:(ob + 1) * P], lambda k: hid[:, k, s], MB)

        @block.vector
        def _(dve):
            own = Own(dve, dve_step)
            V = nc.vector
            for b in range(2):
                V.memset(sq[:, b:b + 1], 0.0).then_inc(free[b], 1)
            for k in range(KB * NH):
                V.memset(smax[:, k:k + 1], 0.0).then_inc(proj_added, 1)
            own.step(V.memset(acc[:], 0.0))
            own.step(V.memset(lg[:, :, NBLK:], BIG))

            dve.wait_ge(small_loaded, 48)
            dve.wait_ge(ada_summed, 1)
            own.step(V.tensor_tensor(
                ada[:].rearrange("p a k b -> p (a k) b"), score[:, 0, 0:12 * B].rearrange("p (a b) -> p a b", b=B),
                v_("ada_b").unsqueeze(2).broadcast_to([P, 12, B]), ALU.add))
            own.wait()
            for c in (SCALE1, SCALE2):
                own.step(V.tensor_scalar(ada[:, c], ada[:, c], 1.0, None, ALU.add))

            def mod(c, k, h):
                nb = HALF // T
                return ada[:, c, k, h * nb:(h + 1) * nb].unsqueeze(2).broadcast_to([P, nb, T])

            def tok(ap):
                return ap.rearrange("p (b t) -> p b t", t=T)

            def norm(src, n, shift, scale):
                h = n % NH
                s = slice(h * HALF, (h + 1) * HALF)
                dve.wait_ge(mean_ready, n + 1)
                if n:
                    dve.wait_ge(square_ready, n)
                for k in range(KB):
                    last = V.tensor_tensor(centred[:, k], src[:, k, s], proj[:, h], ALU.subtract)
                    if k < KB - 1:
                        own.step(last)
                last.then_inc(centred_ready, 1)
                dve.wait_ge(var_ready, n + 1)
                V.tensor_scalar(var[:], proj[:, NH + h], LN_EPS, None, ALU.add).then_inc(var_copied, 1)
                dve.wait_ge(rstd_ready, n + 1)
                own.step(V.reciprocal(rstd[:], std[:]))
                own.wait()
                own.step(V.tensor_tensor(std[:], rstd[:], rstd[:], ALU.mult))
                own.wait()
                own.step(V.scalar_tensor_tensor(std[:], std[:], -0.5, var[:], ALU.mult, ALU.mult))
                own.wait()
                own.step(V.scalar_tensor_tensor(rstd[:], std[:], 1.5, rstd[:], ALU.add, ALU.mult))
                own.wait()
                for k in range(KB):
                    own.step(V.tensor_tensor(x1[:, k, s], centred[:, k], rstd[:], ALU.mult))
                own.wait()
                for k in range(KB):
                    own.step(V.tensor_tensor(tok(x1[:, k, s]), tok(x1[:, k, s]), mod(scale, k, h), ALU.mult))
                own.wait()
                for k in range(KB):
                    last = V.tensor_tensor(tok(x1[:, k, s]), tok(x1[:, k, s]), mod(shift, k, h), ALU.add)
                    if k < KB - 1:
                        own.step(last)
                last.then_inc(x1_ready, 1)

            dve.wait_ge(x_loaded, 32)
            for h in range(NH):
                norm(x_sb, h, SHIFT1, SCALE1)
            own.wait()

            STEPS = QUAD * (NB4 + 3)
            start = own.n
            s8 = score[:].rearrange("p a (g s) -> p (a g) s", g=4)
            with dve.Fori(0, NQUAD) as i:
                own.n, own.base = 0, i * STEPS + start
                for w, name in enumerate(("q_b", "k_b", "v_b")):
                    V.tensor_scalar(pass_b[:, w], vec[:, bass.ds(i * QUAD + VEC[name][0], QUAD)], 1.0, None, ALU.mult
                                    ).then_inc(bias_ready, 1)
                for j in range(QUAD):
                    dve.wait_ge(scores_ready, i * QUAD + j + 1)
                    for q in range(NB4):
                        s = slice(q * T, (q + 1) * T)
                        own.step(V.tensor_reduce(smax[s], s8[s, :, s], AX_X, ALU.max))
                    own.wait()
                    for q in range(NB4):
                        s = slice(q * T, (q + 1) * T)
                        V.tensor_tensor(sc[s], s8[s, :, s], smax[s].unsqueeze(2).broadcast_to([T, G, T]), ALU.subtract
                                        ).then_inc(shifted, 1)
                    dve.wait_ge(exp_ready, i * QUAD + j + 1)
                    own.step(V.tensor_reduce(ssum[:], pe_[:], AX_X, ALU.add))
                    own.wait()
                    own.step(V.reciprocal(srec[:], ssum[:]))
                    own.wait()
                    own.step(V.tensor_tensor(pn[:], pe_[:], srec[:].unsqueeze(2).broadcast_to([P, G, T]), ALU.mult))
                    own.wait()
                    V.transpose(pt[:].rearrange("p g t -> p (g t)"), pn[:].rearrange("p g t -> p (g t)")
                                ).then_inc(pt_ready, 1)
                assert own.n == STEPS
                dve.wait_ge(proj_ready, i + 1)
                for ob in range(KB):
                    for h in range(NH):
                        a = acc[:, ob, h * HALF:(h + 1) * HALF]
                        V.tensor_tensor(a, a, proj[:, ob * NH + h], ALU.add).then_inc(proj_added, 1)
            own.n, own.base = start + NQUAD * STEPS, 0
            dve.wait_ge(proj_added, KB * NH * (NQUAD + 1))

            def gated(dst, src, bias, gate, ob, h, also):
                own.step(V.tensor_scalar(dst, src, bias, None, ALU.add))
                own.wait()
                own.step(V.tensor_tensor(tok(dst), tok(dst), mod(gate, ob, h), ALU.mult))
                own.wait()
                return V.tensor_tensor(dst, dst, also, ALU.add)

            for ob in range(KB):
                for h in range(NH):
                    s = slice(h * HALF, (h + 1) * HALF)
                    last = gated(acc[:, ob, s], acc[:, ob, s], v_("out_b", ob), GATE1, ob, h, x_sb[:, ob, s])
                    if (ob, h) != (KB - 1, NH - 1):
                        own.step(last)
            last.then_inc(proj_added, 1)
            dve.wait_ge(proj_added, KB * NH * (NQUAD + 1) + 1)
            own.wait()
            for h in range(NH):
                norm(acc, NH + h, SHIFT2, SCALE2)

            dve.wait_ge(late_loaded, 9 * 16)
            own.step(V.tensor_copy(coup_parts[0][:], coup_sb[:]))
            own.wait()
            own.step(V.tensor_tensor(coup_rest[:], coup_sb[:], coup_parts[0][:], ALU.subtract))
            own.wait()
            own.step(V.tensor_copy(coup_parts[1][:], coup_rest[:]))
            own.wait()
            own.step(V.tensor_tensor(coup_parts[2][:], coup_rest[:], coup_parts[1][:], ALU.subtract))
            own.step(V.tensor_scalar(hb[:, 0:KB], v_("bz"), 0.5, None, ALU.mult))
            own.wait()
            V.memset(hb[:, KB:2 * KB], 0.0).then_inc(coup_ready, 1)

            def wait_full(use):
                dve.wait_ge(full[bank_of(use)], count_of(use))

            for h in range(NH):
                s = slice(h * HALF, (h + 1) * HALF)
                for ob in range(KB):
                    use = USE_F1[h] + MB + ob
                    wait_full(use)
                    tmp = centred[:, ob]
                    own.step(V.tensor_scalar(tmp, bank[bank_of(use)][:], v_("ffn_b2", ob), None, ALU.add))
                    own.wait()
                    V.tensor_tensor(tok(tmp), tok(tmp), mod(GATE2, ob, h), ALU.mult).then_inc(free[bank_of(use)], 1)
                    dve.wait_ge(free[bank_of(use)], count_of(use) + 1)
                    V.tensor_tensor(acc[:, ob, s], acc[:, ob, s], tmp, ALU.add).then_inc(x3_ready, 1)

            n = 0
            for h in range(NH):
                s = slice(h * HALF, (h + 1) * HALF)
                for ob in range(KB):
                    use = USE_GRU[h] + 2 * ob
                    dve.wait_ge(free[bank_of(use)], count_of(use) + 1)
                    own.step(V.tensor_scalar(za[:], tz[:], -0.5, 0.5, ALU.mult, ALU.add))
                    own.step(V.tensor_scalar(zb, tz[:], 0.5, 0.5, ALU.mult, ALU.add))
                    dve.wait_ge(free[bank_of(use + 1)], count_of(use + 1) + 1)
                    V.tensor_scalar(nneg, nn_[:], 0.0, None, ALU.min).then_inc(gate_in, 1)
                    own.step(V.tensor_scalar(npos[:], nn_[:], 0.0, 0.5, ALU.max, ALU.add))
                    dve.wait_ge(tn_ready, n + 1)
                    own.wait()
                    own.step(V.scalar_tensor_tensor(npos[:], tn[:], 0.5, npos[:], ALU.mult, ALU.add))
                    own.wait()
                    own.step(V.tensor_tensor(zb, zb, npos[:], ALU.mult))
                    own.wait()
                    a0, b0 = tok(za[:])[:, :, 0:1], tok(zb)[:, :, 0:1]
                    own.step(V.scalar_tensor_tensor(b0, a0, 0.5, b0, ALU.mult, ALU.add))
                    own.wait()
                    own.step(V.memset(a0, 0.0))
                    own.wait()
                    own.step(V.tensor_tensor_scan(npos[:], za[:], zb, 0.0, ALU.mult, ALU.add))
                    own.wait()
                    V.tensor_tensor(drive[:, ob, s], x_sb[:, ob, s], npos[:], ALU.add).then_inc(z_used, 1)
                    dve.wait_ge(z_used, n + 1)
                    n += 1
            for ob in range(KB):
                own.step(V.tensor_scalar(dbias[:, :, ob * B:(ob + 1) * B],
                                         drive[:, ob].rearrange("p (b t) -> p t b", t=T), v_("c2_b", ob), None, ALU.add))
            own.step(V.tensor_copy(pst[:, 0], cond_sb[:].rearrange("p k b -> p (k b)")))
            own.wait()
            V.tensor_copy(qst[:, 0], cond_sb[:].rearrange("p k b -> p (k b)")).then_inc(q_ready, 1)
            dve.wait_ge(q_ready, 1)

            H1, H2, H6 = STAGE_H[0], STAGE_H[2], STAGE_H[3]
            RK = 31
            start = own.n
            with dve.Fori(0, T) as t:
                own.n, own.base = 0, t * RK + start
                d_t = dbias[:, bass.ds(t, 1)].rearrange("p a c -> p (a c)")
                V.memset(psum_[:, 0:1], 0.0).then_inc(p_ready, 1)
                own.step(V.scalar_tensor_tensor(qd[:, 0], d_t, H1, qst[:, 0], ALU.mult, ALU.add))
                own.step(V.scalar_tensor_tensor(qd[:, 1], d_t, H2, qst[:, 0], ALU.mult, ALU.add))
                own.wait()
                own.step(V.scalar_tensor_tensor(rp[:], pst[:, 0], -H1, qd[:, 0], ALU.mult, ALU.add))
                for s in range(4):
                    hs = STAGE_H[s]
                    own.step(V.tensor_tensor(sq[:], qst[:, s], qst[:, s], ALU.mult))
                    if s == 3:
                        own.step(V.scalar_tensor_tensor(qsum[:], qst[:, 3], 1.0 / 3.0, qsum[:], ALU.mult, ALU.add))
                    own.wait()
                    own.step(V.scalar_tensor_tensor(cub[:], sq[:], -3.0, qst[:, s], ALU.add, ALU.mult))
                    if s == 3:
                        own.step(V.scalar_tensor_tensor(rp[:], pst[:, 3], -H6, qsum[:], ALU.mult, ALU.add))
                    dve.wait_ge(th32_ready, t * 4 + s + 1)
                    V.tensor_tensor(thlo[:], th32[:], th16[:], ALU.subtract).then_inc(lo_ready, 1)
                    own.wait()
                    own.step(V.scalar_tensor_tensor(base[:], cub[:], -hs / 3.0, rp[:], ALU.mult, ALU.add))
                    own.wait()
                    if s < 3:
                        dve.wait_ge(bp_ready, t * 3 + s + 1)
                        V.scalar_tensor_tensor(pst[:, s + 1], qst[:, s], hs * EPSILON, bp[:], ALU.mult, ALU.add
                                               ).then_inc(p_ready, 1)
                        dve.wait_ge(p_ready, t * 4 + s + 2)
                        if s < 2:
                            own.step(V.scalar_tensor_tensor(rp[:], pst[:, s + 1], -STAGE_H[s + 1], qd[:, s], ALU.mult,
                                                            ALU.add))
                        dve.wait_ge(coupled, t * 4 + s + 1)
                        V.scalar_tensor_tensor(qst[:, s + 1], score[:, 0, 0:KB * B], hs, base[:], ALU.mult, ALU.add
                                               ).then_inc(q_ready, 1)
                        dve.wait_ge(q_ready, t * 4 + s + 2)
                        if s == 0:
                            own.step(V.tensor_tensor(qsum[:], qst[:, 1], qst[:, 0], ALU.subtract))
                            own.step(V.tensor_tensor(psum_[:], pst[:, 1], pst[:, 0], ALU.subtract))
                        if s == 1:
                            own.step(V.scalar_tensor_tensor(qsum[:], qst[:, 2], 2.0, qsum[:], ALU.mult, ALU.add))
                            own.step(V.scalar_tensor_tensor(psum_[:], pst[:, 2], 2.0, psum_[:], ALU.mult, ALU.add))
                            own.wait()
                            own.step(V.tensor_scalar(qsum[:], qsum[:], 1.0 / 3.0, None, ALU.mult))
                            own.step(V.tensor_scalar(psum_[:], psum_[:], 1.0 / 3.0, H6 * EPSILON * ALPHA, ALU.mult,
                                                     ALU.add))
                            own.wait()
                            own.step(V.scalar_tensor_tensor(qsum[:], d_t, H6, qsum[:], ALU.mult, ALU.add))
                        if s == 2:
                            own.step(V.scalar_tensor_tensor(psum_[:], pst[:, 3], 1.0 / 3.0 - H6 * EPSILON * BETA,
                                                            psum_[:], ALU.mult, ALU.add))
                    else:
                        own.step(V.scalar_tensor_tensor(psum_[:], qst[:, 3], H6 * EPSILON, psum_[:], ALU.mult, ALU.add))
                        own.wait()
                        own.step(V.tensor_scalar(pst[:, 0], psum_[:], CLAMP, -CLAMP, ALU.min, ALU.max))
                        dve.wait_ge(coupled, t * 4 + 4)
                        own.step(V.scalar_tensor_tensor(qn[:], score[:, 0, 0:KB * B], H6, base[:], ALU.mult, ALU.add))
                        own.wait()
                        own.step(V.tensor_scalar(trace[:, :, bass.ds(t, 1), :].rearrange("p k a b -> p (k a) b"),
                                                 qn[:].rearrange("p (k b) -> p k b", k=KB), CLAMP, -CLAMP,
                                                 ALU.min, ALU.max))
                        V.tensor_scalar(qst[:, 0], qn[:], CLAMP, -CLAMP, ALU.min, ALU.max).then_inc(q_ready, 1)
                        dve.wait_ge(q_ready, t * 4 + 5)
                        own.wait()
                assert own.n == RK, own.n
            own.n, own.base = start + T * RK, 0

            dve.wait_ge(logits_ready, 1)
            own.step(V.tensor_tensor(lg[:, :, 0:NBLK], score[:, 1, 0:G * NBLK].rearrange("p (g c) -> p g c", g=G),
                                     br_sb[:].unsqueeze(1).broadcast_to([P, G, NBLK]), ALU.add))
            own.wait()
            for g in range(G):
                own.step(V.max(top8[:, g], lg[:, g]))
            own.wait()
            for g in range(G):
                own.step(V.match_replace(lgr[:, g], top8[:, g], lg[:, g], -BIG))
            own.wait()
            own.step(V.tensor_scalar(mask[:], lgr[:, :, 0:NBLK], -BIG, None, ALU.is_equal))
            own.wait()
            for g in range(G):
                V.tensor_copy(maskx[:, g].rearrange("p (c r) -> p c r", c=NBLK),
                              mask[:, g].unsqueeze(2).broadcast_to([P, NBLK, MLP // NBLK])).then_inc(mask_ready, 1)
            n = 0
            for h in range(NH):
                s = slice(h * HALF, (h + 1) * HALF)
                for m in range(MB):
                    use = USE_G1[h] + m
                    dve.wait_ge(free[bank_of(use)], count_of(use) + 1)
                    dve.wait_ge(maskb_ready, n + 1)
                    V.tensor_tensor(hid[:, m, s], hid[:, m, s], proj[:, n % 4], ALU.mult).then_inc(h_ready, 1)
                    n += 1
                    dve.wait_ge(h_ready, n)
                    V.memset(smax[:, 0:1], 0.0).then_inc(maskb_used, 1)
                for ob in range(KB):
                    use = USE_G1[h] + MB + ob
                    wait_full(use)
                    V.tensor_tensor(osb[:, ob, s].rearrange("p (t b) -> p t b", b=B),
                                    bank[bank_of(use)][:].rearrange("p (t b) -> p t b", b=B),
                                    drive[:, ob].rearrange("p (b t) -> p t b", t=T)[:, h * T // 2:(h + 1) * T // 2],
                                    ALU.add).then_inc(out_ready, 1)
                    if h == 0:
                        dve.wait_ge(out_ready, ob + 1)
                        V.memset(smax[:, 1:2], 0.0).then_inc(free[bank_of(use)], 1)


def kernel(**inputs):
    import numpy as np
    import concourse.bacc as bacc
    from concourse.bass_utils import run_bass_kernel_spmd

    a = {k: np.asarray(v) for k, v in inputs.items()}

    def rows(w, *shape):
        return w.reshape(-1, P, *w.shape[1:]).swapaxes(0, 1).reshape(P, -1, *(shape or w.shape[1:]))

    def column(v):
        return v.reshape(-1, P).T

    qkv = a["L0_cond_qkv_w"].reshape(KB, P, 3, H, DH)
    arrays = {
        "xT": rows(a["x"].transpose(2, 0, 1).reshape(D, N)),
        "condT": rows(a["cond_2048"].T),
        "ada_w": rows(a["L0_cond_ada_w"]),
        "vecs": np.concatenate([column(v) for v in (
            a["L0_cond_ada_b"], *a["L0_cond_qkv_b"].reshape(3, -1), a["L0_cond_out_b"], a["L0_cond_ffn_b1"],
            a["L0_cond_ffn_b2"], a["L0_attn_bz"], a["L0_attn_bn"], a["L0_cond2_bias"])], axis=1),
        "br": np.repeat(a["L0_ffn_br"][None], P, axis=0),
        "wqk": qkv[:, :, 0:2].transpose(3, 1, 0, 2, 4),
        "wv": qkv[:, :, 2].reshape(KB, P, NQUAD, QUAD * DH).transpose(2, 1, 0, 3),
        "wo": a["L0_cond_out_w"].reshape(H, DH, D).transpose(1, 0, 2),
        "ffn_w1": rows(a["L0_cond_ffn_w1"]),
        "ffn_w2": rows(a["L0_cond_ffn_w2"]),
        "wzT": rows(a["L0_attn_Wz"].T),
        "wnT": rows(a["L0_attn_Wn"].T),
        "coupT": rows(a["L0_cond2_coupling"].T),
        "wrT": rows(a["L0_ffn_Wr"].T),
        "w1T": rows(a["L0_ffn_W1"].T),
        "w2T": rows(a["L0_ffn_W2"].T),
    }
    arrays = {k: np.ascontiguousarray(v) for k, v in arrays.items()}
    nc = bacc.Bacc("TRN2", target_bir_lowering=False, num_devices=1)
    args = [nc.dram_tensor(k, v.shape, mybir.dt.from_np(v.dtype), kind="ExternalInput").ap() for k, v in arrays.items()]
    out = nc.dram_tensor("out_0_dram", (P, KB, N), F32, kind="ExternalOutput").ap()
    build(nc, *args, out)
    r = run_bass_kernel_spmd(nc, [arrays], core_ids=[0])
    got = r.results[0]["out_0_dram"].reshape(P, KB, T, B)
    return np.ascontiguousarray(got.transpose(3, 2, 1, 0).reshape(B, T, D))
```

```python
from contextlib import ExitStack

import concourse.bass as bass
from concourse import mybir

ALU = mybir.AluOpType
ACT = mybir.ActivationFunctionType
F32 = mybir.dt.float32
F16 = mybir.dt.float16
BF16 = mybir.dt.bfloat16
AX_X = mybir.AxisListType.X

P = 128
B, T, D = 32, 32, 256
N = B * T
KB = D // P
H, DH = 16, 128
QUAD = 4
NQUAD = H // QUAD
HALF = N // 2
NH = N // HALF
G = N // P
NB4 = P // T
MLP = 4 * D
MB = MLP // P
NBLK, TOPK = 16, 4
LN_EPS = 1e-6
SCALE = float(DH) ** -0.5
DT, EPSILON, ALPHA, BETA, CLAMP = 0.01, 0.08, 0.7, 0.8, 20.0
UNROLL = 4
STAGE_H = (0.5 * DT, 0.5 * DT, DT, DT / 6.0)
BIG = 3.0e38

VEC = {}
_at = 0
for _name, _n in (("ada_b", 12), ("q_b", H), ("k_b", H), ("v_b", H), ("out_b", KB), ("ffn_b1", MB), ("ffn_b2", KB),
                  ("bz", KB), ("bn", KB), ("c2_b", KB)):
    VEC[_name] = (_at, _at + _n)
    _at += _n
NVEC = _at

SHIFT1, SCALE1, GATE1, SHIFT2, SCALE2, GATE2 = range(6)

NBANK = 5
USE_PROJ = [0, 10, 16, 22]
USE_V = [4, 5, 6, 7, 8, 9, 14, 15]
USE_PV = [20, 26, 30, 35]
USE_OUT = [[28, 29, 32, 37], [33, 34, 38, 39]]
USES_PER_PASS = 40
SPLIT_ORDER = [("qk", 0), ("v", 0), ("v", 1), ("qk", 1), ("qk", 2), ("o", 0), ("o", 1), ("qk", 3)]
WSCALE = 16.0


def build(nc, xT, condT, ada_w, vecs, br, wqk, wv, wo, ffn_w1, ffn_w2, wzT, wnT, coupT, wrT, w1T, w2T, out):
    with ExitStack() as ctx:
        def sb(name, shape, dt=F32):
            return ctx.enter_context(nc.sbuf_tensor(name, shape, dt))

        def sem(name):
            return ctx.enter_context(nc.semaphore(name))

        bank = [ctx.enter_context(nc.psum_tensor(f"bank{i}", [P, 512], F32)) for i in range(NBANK)]
        score = ctx.enter_context(nc.psum_tensor("score", [P, 2, 512], F32))
        spare = ctx.enter_context(nc.psum_tensor("spare", [P, 512], F32))

        x_sb = sb("x_sb", [P, KB, N])
        cond_sb = sb("cond_sb", [P, KB, B])
        adaw_sb = sb("adaw_sb", [P, KB, 6 * D])
        vec = sb("vec", [P, NVEC])
        br_sb = sb("br_sb", [P, NBLK])
        wqk_sb = sb("wqk_sb", [P, QUAD, KB, 2, DH])
        wv_sb = sb("wv_sb", [P, KB, QUAD * DH])
        wo_sb = sb("wo_sb", [P, QUAD, D])
        f1_sb = sb("f1_sb", [P, KB, MLP])
        f2_sb = sb("f2_sb", [P, MB, D])
        wz_sb = sb("wz_sb", [P, KB, D])
        wn_sb = sb("wn_sb", [P, KB, D])
        coup_sb = sb("coup_sb", [P, KB, D])
        coup_rest = sb("coup_rest", [P, KB, D])
        coup_parts = [sb(f"coup_part{i}", [P, KB, D], BF16) for i in range(3)]
        wr_sb = sb("wr_sb", [P, KB, NBLK])
        w1_sb = sb("w1_sb", [P, KB, MLP])
        w2_sb = sb("w2_sb", [P, MB, D])

        ones = sb("ones", [P, P])
        ident = sb("ident", [P, P], BF16)

        ada = sb("ada", [P, 6, KB, B])
        centred = sb("centred", [P, KB, HALF])
        square = sb("square", [P, KB, HALF])
        var = sb("var", [P, NH, HALF])
        newton = coup_rest[:].rearrange("p k n -> p (k n)")
        rstd = sb("rstd", [P, NH, HALF])
        eps = sb("eps", [P, 1])
        x1 = sb("x1", [P, KB, N])

        big = sb("big", [P, 2 * 4096])
        qk_sb = big[:, 0:4096].bitcast(F16).rearrange("p (r w c n) -> p r w c n", r=2, w=2, c=2)
        v_sb = big[:, 4096:8192].bitcast(F16).rearrange("p (g c n) -> p g c n", g=G, c=2)
        hid = big[:, :].rearrange("p (m n) -> p m n", m=MB)
        hid_of = big[:, :].rearrange("p (s m n) -> p s m n", s=G, m=MB)
        ao_sb = sb("ao_sb", [P, QUAD, N])
        ao_pair = ao_sb[:].rearrange("p j n -> p (j n)").bitcast(F16).rearrange("p (j c n) -> p j c n", j=QUAD, c=2)
        x1_pair = x1[:].rearrange("p k n -> p (k n)").bitcast(F16).rearrange("p (c k n) -> p c k n", c=2, k=KB)
        pairs_sb = adaw_sb[:].rearrange("p k n -> p (k n)").bitcast(F16)
        wqk_pair = pairs_sb[:, 0:2048].rearrange("p (r c n) -> p r c n", r=2, c=2)
        wv_pair = pairs_sb[:, 2048:4096].rearrange("p (c k n) -> p c k n", c=2, k=KB)
        wo_pair = pairs_sb[:, 4096:6144].rearrange("p (c j n) -> p c j n", c=2, j=QUAD)
        pass_b = sb("pass_b", [P, 3, QUAD])
        smax = sb("smax", [P, G])
        ssum = sb("ssum", [P, G])
        srec = sb("srec", [P, G])
        sc = sb("sc", [P, G, T])
        pe_ = sb("pe_", [P, G, T])
        pn = sb("pn", [P, G, T])
        pt = sb("pt", [P, G, T])
        sraw = sb("sraw", [P, G, T])
        ptx = sb("ptx", [P, 2, G, P], F16)
        acc = sb("acc", [P, KB, N])

        hb = sb("hb", [P, KB])
        tz = sb("tz", [P, HALF])
        wscale = tz
        nn_ = sb("nn_", [P, HALF])
        nneg = square[:, 0]
        tn = sb("tn", [P, HALF])
        npos = sb("npos", [P, HALF])
        za = sb("za", [P, HALF])
        zb = square[:, 1]
        centred_of = ((centred[:, 0], centred[:, 1]), (nn_[:], tn[:]))
        square_of = ((square[:, 0], square[:, 1]), (npos[:], za[:]))
        drive = sb("drive", [P, KB, N])
        dbias = sb("dbias", [P, T, KB * B])

        qp = sb("qp", [P, 4, 2 * KB * B])
        padded = adaw_sb[:].rearrange("p k n -> p (k n)")[:, 0:KB * (T + UNROLL) * B].rearrange(
            "p (k t b) -> p k t b", k=KB, t=T + UNROLL)
        trace = padded[:, :, UNROLL - 1:]
        q_group = centred[:, 0, 0:KB * P].rearrange("p (k n) -> p k n", k=KB)
        th16 = sb("th16", [P, KB * B], F16)
        th32 = sb("th32", [P, KB * B])
        thlo = sb("thlo", [P, KB * B], F16)
        sq = sb("sq", [P, KB * B])
        cub = sb("cub", [P, KB * B])
        base = sb("base", [P, KB * B])
        qd = sb("qd", [P, 2, KB * B])
        pc = sb("pc", [P, 3, KB * B])
        pfac = sb("pfac", [P, 6, KB * B])
        pterm = sb("pterm", [P, 2, KB * B])
        bp = sb("bp", [P, KB * B])
        lin = sb("lin", [P, 2, KB * B])
        lin4 = sb("lin4", [P, KB * B])
        d6 = sb("d6", [P, KB * B])
        comb = sb("comb", [P, KB * B])
        pacc = sb("pacc", [P, KB * B])
        pend = sb("pend", [P, KB * B])
        qn = sb("qn", [P, KB * B])

        lg = sb("lg", [P, G, NBLK + TOPK])
        top8 = sb("top8", [P, G, 8])
        lgr = sb("lgr", [P, G, NBLK + TOPK])
        mask = sb("mask", [P, G, NBLK], BF16)
        maskx = ao_sb[:].rearrange("p j n -> p (j n)").bitcast(BF16).rearrange("p (g n) -> p g n", g=G)
        osb = x1

        def v_(name, j=None):
            a, b = VEC[name]
            return vec[:, a:b] if j is None else vec[:, a + j:a + j + 1]

        x_loaded = [sem(f"x_loaded{h}") for h in range(NH)]
        small_loaded = sem("small_loaded")
        late_loaded = sem("late_loaded")
        qk_loaded = [sem(f"qk_loaded{j}") for j in range(QUAD)]
        v_loaded = sem("v_loaded")
        o_loaded = sem("o_loaded")
        ones_ready = sem("ones_ready")
        ident_ready = sem("ident_ready")
        ada_summed = sem("ada_summed")
        ada_ready = sem("ada_ready")
        mean_ready = sem("mean_ready")
        var_ready = sem("var_ready")
        centred_ready = sem("centred_ready")
        square_ready = sem("square_ready")
        var_copied = sem("var_copied")
        rstd_ready = sem("rstd_ready")
        x1_ready = sem("x1_ready")
        dve_step = sem("dve_step")
        pool_step = sem("pool_step")
        act_step = sem("act_step")
        full = [sem(f"full{i}") for i in range(NBANK)]
        free = [sem(f"free{i}") for i in range(NBANK)]
        bias_ready = sem("bias_ready")
        scores_ready = sem("scores_ready")
        high_ready = sem("high_ready")
        shifted = sem("shifted")
        exp_ready = sem("exp_ready")
        pt_ready = sem("pt_ready")
        ptx_cleared = sem("ptx_cleared")
        scores_copied = sem("scores_copied")
        high_placed = sem("high_placed")
        ptx_ready = sem("ptx_ready")
        eps_ready = sem("eps_ready")
        normed = sem("normed")
        x1_high_ready = sem("x1_high_ready")
        scaled_ready = sem("scaled_ready")
        w_high_ready = sem("w_high_ready")
        split_ready = sem("split_ready")
        x2_ready = sem("x2_ready")
        coup_ready = sem("coup_ready")
        hid_ready = sem("hid_ready")
        x3_ready = sem("x3_ready")
        gate_in = sem("gate_in")
        gate_th = sem("gate_th")
        z_ready = sem("z_ready")
        z_used = sem("z_used")
        tn_ready = sem("tn_ready")
        drive_ready = sem("drive_ready")
        q_ready = sem("q_ready")
        clip_ready = sem("clip_ready")
        pacc_ready = sem("pacc_ready")
        trace_done = sem("trace_done")
        th16_ready = sem("th16_ready")
        th32_ready = sem("th32_ready")
        lo_ready = sem("lo_ready")
        coupled = sem("coupled")
        p_ready = sem("p_ready")
        bp_ready = sem("bp_ready")
        logits_ready = sem("logits_ready")
        mask_ready = sem("mask_ready")
        maskb_ready = sem("maskb_ready")
        hidden_ready = sem("hidden_ready")
        gelu_ready = sem("gelu_ready")
        h_ready = sem("h_ready")
        out_ready = sem("out_ready")
        stored = sem("stored")

        AFTER = NQUAD * USES_PER_PASS
        USE_F1 = [AFTER, AFTER + MB + KB]
        USE_GRU = [AFTER + 2 * MB + KB, AFTER + 2 * (MB + KB) + 2 * KB]
        USE_F2 = [AFTER + MB, AFTER + 2 * MB + KB + 2 * KB]
        USE_G2 = [AFTER + 2 * (MB + KB) + 2 * KB * NH + KB * h for h in range(NH)]
        LAST = [(slice(G // 2, G), list(range(G // 2 - 1, G - 1))), (slice(0, G // 2), [G - 1, *range(G // 2 - 1)])]
        FIRST_HIDDEN = 4
        GELU_AT = (9, 13)
        LOGITS_AT = 14

        def bank_of(use):
            return use % NBANK

        def count_of(use, start=0):
            return start * (USES_PER_PASS // NBANK) + use // NBANK + 1

        NPAR = USES_PER_PASS // NBANK
        NSPLIT = len(SPLIT_ORDER)

        def split_arrays(kind, part):
            if kind == "qk":
                return wqk_sb[:, part].rearrange("p k w d -> p (k w d)"), wqk_pair[:, part % 2]
            if kind == "v":
                return wv_sb[:, part], wv_pair[:, :, part]
            o = slice(part * QUAD // 2, (part + 1) * QUAD // 2)
            return wo_sb[:, o].rearrange("p j n -> p (j n)"), wo_pair[:, :, o].rearrange("p c j n -> p c (j n)")

        class Own:

            def __init__(self, eng, semaphore):
                self.eng, self.sem, self.n, self.base = eng, semaphore, 0, 0

            def step(self, ins):
                ins.then_inc(self.sem, 1)
                self.n += 1

            def wait(self):
                self.eng.wait_ge(self.sem, self.base + self.n)

        def runs(groups):
            out_runs, first = [], 0
            for n in range(1, len(groups) + 1):
                if n == len(groups) or groups[n] != groups[n - 1] + 1:
                    out_runs.append((groups[first], groups[n - 1] + 1))
                    first = n
            return out_runs

        def mask_bank(n):
            return (spare[:], score[:, 0], score[:, 1])[n % 3]

        s8 = score[:].rearrange("p a (g s) -> p (a g) s", g=4)
        block = ctx.enter_context(nc.Block())

        @block.sync
        def _(sp):
            for h in range(NH):
                s = slice(h * HALF, (h + 1) * HALF)
                sp.dma_start(x_sb[:, :, s], xT[:, :, s]).then_inc(x_loaded[h], 16)
            for j in range(QUAD):
                sp.dma_start(wqk_sb[:, j], wqk[j]).then_inc(qk_loaded[j], 16)
            sp.dma_start(wv_sb[:], wv[0]).then_inc(v_loaded, 16)
            sp.dma_start(wo_sb[:], wo[:, 0:QUAD]).then_inc(o_loaded, 16)
            with sp.Fori(0, NQUAD - 1) as i:
                for t, (kind, part) in enumerate(SPLIT_ORDER):
                    if (kind, part) in (("v", 0), ("o", 0)):
                        continue
                    sp.wait_ge(split_ready, i * NSPLIT + t + 1)
                    if kind == "qk":
                        sp.dma_start(wqk_sb[:, part],
                                     wqk[bass.ds(i * QUAD + QUAD + part, 1)].rearrange("a p k w d -> (a p) k w d")
                                     ).then_inc(qk_loaded[part], 16)
                    elif kind == "v":
                        sp.dma_start(wv_sb[:], wv[bass.ds(i + 1, 1)].rearrange("a p k n -> (a p) k n")
                                     ).then_inc(v_loaded, 16)
                    else:
                        sp.dma_start(wo_sb[:], wo[:, bass.ds(i * QUAD + QUAD, QUAD)]).then_inc(o_loaded, 16)
            n = 0
            for _, groups in LAST:
                for ob in range(KB):
                    for a, b in runs(groups):
                        n += 1
                        sp.wait_ge(out_ready, n)
                        sp.dma_start(out[:, ob, a * P:b * P], osb[:, ob, a * P:b * P]).then_inc(stored, 16)
            sp.wait_ge(stored, 16 * n)

        @block.gpsimd
        def _(pool):
            own = Own(pool, pool_step)
            nc.gpsimd.memset(ones[:], 1.0 / D).then_inc(ones_ready, 1)
            own.step(nc.gpsimd.memset(ident[:], 0.0))
            own.wait()
            nc.gpsimd.affine_select(out=ident[:], in_=ident[:], compare_op=ALU.not_equal, fill=1.0, base=0,
                                    pattern=[[-1, P]], channel_multiplier=1).then_inc(ident_ready, 1)
            own.step(nc.gpsimd.memset(ptx[:], 0.0))
            own.step(nc.gpsimd.memset(wscale[:], WSCALE))
            for s, f in enumerate((*(-BETA * h * EPSILON for h in STAGE_H[0:3]), 2.0,
                                   1.0 - 3.0 * BETA * STAGE_H[3] * EPSILON, 1.0 / 3.0)):
                own.step(nc.gpsimd.memset(pfac[:, s], f))

            own.wait()
            nc.gpsimd.drain().then_inc(ptx_cleared, 1)
            with pool.Fori(0, NQUAD) as i:
                def scale(t):
                    kind, part = SPLIT_ORDER[t]
                    loaded = {"qk": qk_loaded[part % QUAD], "v": v_loaded, "o": o_loaded}[kind]
                    w, _ = split_arrays(kind, part)
                    pool.wait_ge(loaded, i * 16 + 16)
                    nc.gpsimd.tensor_tensor(w, w, wscale[:], ALU.mult).then_inc(scaled_ready, 1)

                def split(t):
                    w, pair = split_arrays(*SPLIT_ORDER[t])
                    pool.wait_ge(w_high_ready, i * NSPLIT + t + 1)
                    nc.gpsimd.tensor_tensor(pair[:, 1], w, pair[:, 0], ALU.subtract).then_inc(split_ready, 1)

                def place_low(j):
                    for q in range(NB4):
                        s = slice(q * T, (q + 1) * T)
                        pool.wait_ge(high_placed, i * (QUAD * NB4) + NB4 * j + q + 1)
                        nc.gpsimd.tensor_tensor(ptx[s, 1, :, s], pt[s], ptx[s, 0, :, s], ALU.subtract
                                                ).then_inc(ptx_ready, 1)

                scale(0)
                for t in range(NSPLIT):
                    if t + 1 < NSPLIT:
                        scale(t + 1)
                    split(t)
                    if t == 3:
                        pool.wait_ge(split_ready, i * NSPLIT + t + 1)
                        place_low(0)
                        pool.wait_ge(ptx_ready, i * (QUAD * NB4) + NB4)
                pool.wait_ge(split_ready, i * NSPLIT + NSPLIT)
                for j in range(1, QUAD):
                    place_low(j)
                pool.wait_ge(ptx_ready, i * (QUAD * NB4) + QUAD * NB4)
            pool.wait_ge(ptx_ready, NQUAD * QUAD * NB4)
            start = own.n
            gt = nc.gpsimd.tensor_tensor
            with pool.Fori(0, T // UNROLL) as i:
                own.n, own.base = 0, i * (11 * UNROLL) + start

                def p_(s):
                    return qp[:, s, KB * B:]

                for u, s in ((u, s) for u in range(UNROLL) for s in range(4)):
                    pool.wait_ge(p_ready, i * (4 * UNROLL) + 4 * u + s + 1)
                    if s < 3:
                        own.step(gt(bp[:], p_(s), pfac[:, s], ALU.mult))
                        if s == 0:
                            own.step(nc.gpsimd.tensor_scalar(pc[:, 0], p_(0), STAGE_H[0] * EPSILON * ALPHA, None, ALU.add))
                        own.wait()
                        gt(bp[:], bp[:], pc[:, s // 2], ALU.add).then_inc(bp_ready, 1)
                    if s == 0:
                        own.step(nc.gpsimd.tensor_scalar(pc[:, 1], p_(0), STAGE_H[2] * EPSILON * ALPHA, None, ALU.add))
                        own.step(nc.gpsimd.tensor_scalar(pc[:, 2], p_(0), -3.0 * STAGE_H[3] * EPSILON * ALPHA, None,
                                                         ALU.add))
                    if s == 1:
                        own.step(gt(pacc[:], p_(1), pc[:, 2], ALU.subtract))
                    if s >= 2:
                        own.step(gt(pterm[:, s - 2], p_(s), pfac[:, s + 1], ALU.mult))
                        own.wait()
                        own.step(gt(pacc[:], pacc[:], pterm[:, s - 2], ALU.add))
                    if s == 3:
                        own.wait()
                        gt(pacc[:], pacc[:], pfac[:, 5], ALU.mult).then_inc(pacc_ready, 1)
                assert own.n == 11 * UNROLL, own.n

        @block.scalar
        def _(act):
            own = Own(act, act_step)
            act.dma_start(cond_sb[:], condT).then_inc(small_loaded, 16)
            act.dma_start(adaw_sb[:], ada_w).then_inc(small_loaded, 16)
            act.dma_start(vec[:], vecs).then_inc(small_loaded, 16)
            for dst, src in ((br_sb, br), (f1_sb, ffn_w1), (f2_sb, ffn_w2), (wz_sb, wzT), (wn_sb, wnT),
                             (coup_sb, coupT), (wr_sb, wrT), (w1_sb, w1T), (w2_sb, w2T)):
                act.dma_start(dst[:], src).then_inc(late_loaded, 16)

            def squares(n):
                for k in range(KB):
                    act.wait_ge(centred_ready, n * KB + k + 1)
                    nc.scalar.activation(square_of[n % NH][k], centred_of[n % NH][k], ACT.Square).then_inc(square_ready, 1)

            def logs(n):
                h = n % NH
                act.wait_ge(var_ready, n + 1)
                nc.scalar.activation(var[:, h], spare[:], ACT.Identity, bias=eps[:]).then_inc(var_copied, 1)
                act.wait_ge(var_copied, n + 1)
                own.step(nc.scalar.activation(rstd[:, h], var[:, h], ACT.Ln))

            def roots(n):
                nc.scalar.activation(rstd[:, n % NH], rstd[:, n % NH], ACT.Exp, scale=-0.5).then_inc(rstd_ready, 1)

            def x1_high(h):
                for k in range(KB):
                    s = slice(h * HALF, (h + 1) * HALF)
                    act.wait_ge(normed, h * KB + k + 1)
                    nc.scalar.activation(x1_pair[:, 0, k, s], drive[:, k, s], ACT.Copy).then_inc(x1_high_ready, 1)

            act.wait_ge(eps_ready, 1)
            for h in range(NH):
                squares(h)
            for h in range(NH):
                logs(h)
            own.wait()
            for h in range(NH):
                roots(h)
            for h in range(NH):
                x1_high(h)

            act.wait_ge(ptx_cleared, 1)
            with act.Fori(0, NQUAD) as i:
                def high(use, dst, bias=None):
                    act.wait_ge(full[bank_of(use)], i * NPAR + count_of(use))
                    src = bank[bank_of(use)][:]
                    if bias is None:
                        ins = nc.scalar.activation(dst, src, ACT.Copy)
                    else:
                        ins = nc.scalar.activation(dst, src, ACT.Identity, bias=bias)
                    ins.then_inc(high_ready, 1)

                def head_bias(name, j):
                    return pass_b[:, ("q_b", "k_b", "v_b").index(name), j:j + 1]

                def empty_proj(j, k):
                    h, w = k // 2, k % 2
                    high(USE_PROJ[j] + k, qk_sb[:, j % 2, w, 0, h * HALF:(h + 1) * HALF],
                         head_bias(("q_b", "k_b")[w], j))

                def empty_pv(j):
                    for h in range(NH):
                        high(USE_PV[j] + h, ao_pair[:, j, 0, h * HALF:(h + 1) * HALF], head_bias("v_b", j))

                def weights_high(t):
                    w, pair = split_arrays(*SPLIT_ORDER[t])
                    act.wait_ge(scaled_ready, i * NSPLIT + t + 1)
                    nc.scalar.activation(pair[:, 0], w, ACT.Copy).then_inc(w_high_ready, 1)

                def exps(j):
                    act.wait_ge(shifted, i * QUAD + j + 1)
                    nc.scalar.activation(pe_[:], sc[:], ACT.Exp, scale=SCALE / WSCALE ** 2).then_inc(exp_ready, 1)

                def copy_scores(j):
                    act.wait_ge(scores_ready, i * QUAD + j + 1)
                    for q in range(NB4):
                        s = slice(q * T, (q + 1) * T)
                        nc.scalar.activation(sraw[s], s8[s, :, s], ACT.Copy).then_inc(scores_copied, 1)

                def place_high(j):
                    act.wait_ge(pt_ready, i * QUAD + j + 1)
                    for q in range(NB4):
                        s = slice(q * T, (q + 1) * T)
                        nc.scalar.activation(ptx[s, 0, :, s], pt[s], ACT.Copy).then_inc(high_placed, 1)

                def empty_projs(j, ks=range(4)):
                    for k in ks:
                        empty_proj(j, k)

                def empty_values(*gs):
                    for g in gs:
                        high(USE_V[g], v_sb[:, g, 0])

                for t in range(4):
                    weights_high(t)
                act.wait_ge(bias_ready, i * 3 + 3)
                empty_projs(0)
                empty_values(0, 1)
                copy_scores(0)
                empty_values(2)
                exps(0)
                empty_values(3, 4)
                place_high(0)
                weights_high(4)
                empty_values(5)
                empty_projs(1, (0, 1))
                weights_high(5)
                empty_projs(1, (2, 3))
                weights_high(6)
                empty_values(6, 7)
                copy_scores(1)
                empty_projs(2, [0])
                exps(1)
                empty_projs(2, [1])
                weights_high(7)
                empty_projs(2, (2, 3))
                empty_pv(0)
                place_high(1)
                copy_scores(2)
                empty_projs(3, [0])
                exps(2)
                empty_projs(3, (1, 2, 3))
                empty_pv(1)
                place_high(2)
                copy_scores(3)
                exps(3)
                empty_pv(2)
                place_high(3)
                empty_pv(3)

            def empty(use, dst, func, bias=0.0, scale=1.0):
                act.wait_ge(full[bank_of(use)], count_of(use))
                nc.scalar.activation(dst, bank[bank_of(use)][:], func, bias=bias, scale=scale
                                     ).then_inc(free[bank_of(use)], 1)

            for h in range(NH):
                squares(NH + h)
            for h in range(NH):
                logs(NH + h)
                own.wait()
                roots(NH + h)
            for h in range(NH):
                for m in range(MB):
                    empty(USE_F1[h] + m, hid[:, m, h * HALF:(h + 1) * HALF], ACT.Gelu, bias=v_("ffn_b1", m))
            act.wait_ge(coup_ready, 1)
            n = 0
            for h in range(NH):
                for ob in range(KB):
                    use = USE_GRU[h] + 2 * ob
                    if n:
                        act.wait_ge(z_used, n)
                    empty(use, tz[:], ACT.Tanh, bias=hb[:, ob:ob + 1], scale=0.5)
                    empty(use + 1, nn_[:], ACT.Identity, bias=v_("bn", ob))
                    act.wait_ge(gate_in, n + 1)
                    nc.scalar.activation(tn[:], nneg, ACT.Tanh, scale=0.5).then_inc(tn_ready, 1)
                    n += 1

            with act.Fori(0, T // UNROLL) as i:
                for u, s in ((u, s) for u in range(UNROLL) for s in range(4)):
                    act.wait_ge(q_ready, i * (4 * UNROLL) + 4 * u + s + 1)
                    src = qp[:, s, 0:KB * B] if s else qn[:]
                    nc.scalar.activation(th16[:], src, ACT.Tanh).then_inc(th16_ready, 1)
                    nc.scalar.activation(th32[:], src, ACT.Tanh).then_inc(th32_ready, 1)
                    if s == 1:
                        nc.scalar.activation(
                            padded[:, :, bass.ds(i * UNROLL + u + UNROLL - 1, 1), :].rearrange("p k a b -> p (k a) b"),
                            qp[:, 0, 0:KB * B].rearrange("p (k b) -> p k b", k=KB), ACT.Copy).then_inc(trace_done, 1)
                    if (u, s) == (0, 3):
                        nc.scalar.activation(q_group.rearrange("p k (t b) -> p k t b", b=B),
                                             padded[:, :, bass.ds(i * UNROLL, UNROLL), :], ACT.Copy)
                    if 4 * u + s == LOGITS_AT:
                        nc.scalar.activation(lg[:, bass.ds(i, 1), 0:NBLK].rearrange("p a c -> p (a c)"),
                                             score[:, 1, 0:NBLK], ACT.Copy)
                    if 4 * u + s in GELU_AT:
                        half = GELU_AT.index(4 * u + s)
                        nc.scalar.activation(
                            hid_of[:, bass.ds(i, 1), half * 4:(half + 1) * 4].rearrange("p a m n -> p (a m n)"),
                            bank[half][:], ACT.Gelu)

            for half in range(2):
                act.wait_ge(hidden_ready, half + 1)
                nc.scalar.activation(hid_of[:, 0, half * 4:(half + 1) * 4].rearrange("p m n -> p (m n)"), bank[half][:],
                                     ACT.Gelu).then_inc(gelu_ready, 1)

        @block.tensor
        def _(pe):
            def mm(dst, lhsT, rhs, start, stop, **kw):
                return nc.tensor.matmul(dst, lhsT, rhs, start=start, stop=stop, **kw)

            def parts3(dst, a, b):
                return sum3(dst, ((a, b),))

            def sum3(dst, operands, start=True, stop=True):
                for n, (a, b) in enumerate(operands):
                    mm(dst, a[:, 0], b[:, 0], start and n == 0, False)
                    mm(dst, a[:, 0], b[:, 1], False, False)
                    last = mm(dst, a[:, 1], b[:, 0], False, stop and n == len(operands) - 1)
                return last

            def mean_of(src, n):
                h = n % NH
                for k in range(KB):
                    last = mm(score[:, h], ones[:], src[:, k, h * HALF:(h + 1) * HALF], k == 0, k == KB - 1)
                last.then_inc(mean_ready, 1)

            def var_of(n):
                if n:
                    pe.wait_ge(var_copied, n)
                for k in range(KB):
                    pe.wait_ge(square_ready, n * KB + k + 1)
                    last = mm(spare[:], ones[:], square_of[n % NH][k], k == 0, k == KB - 1)
                last.then_inc(var_ready, 1)

            pe.wait_ge(ones_ready, 1)
            for h in range(NH):
                pe.wait_ge(x_loaded[h], 16)
                mean_of(x_sb, h)
            for h in range(NH):
                var_of(h)
            pe.wait_ge(small_loaded, 48)
            for c in range(6 * KB):
                for k in range(KB):
                    last = mm(bank[0][:, c * B:(c + 1) * B], adaw_sb[:, k, c * P:(c + 1) * P], cond_sb[:, k],
                              k == 0, k == KB - 1)
            last.then_inc(ada_summed, 1)
            pe.wait_ge(x1_ready, NH)

            with pe.Fori(0, NQUAD) as i:
                def fill(use):
                    pe.wait_ge(free[bank_of(use)], i * NPAR + count_of(use))
                    return bank[bank_of(use)]

                def taken(use):
                    pe.wait_ge(free[bank_of(use)], i * NPAR + count_of(use) + 1)

                def project(j):
                    pe.wait_ge(split_ready, i * NSPLIT + SPLIT_ORDER.index(("qk", j)) + 1)
                    weights = wqk_pair[:, j % 2].rearrange("p c (k w d) -> p c k w d", k=KB, w=2)
                    for h in range(NH):
                        for w in range(2):
                            use = USE_PROJ[j] + h * 2 + w
                            dst = fill(use)
                            sum3(dst[:], [(weights[:, :, k, w], x1_pair[:, :, k, h * HALF:(h + 1) * HALF])
                                          for k in range(KB)]).then_inc(full[bank_of(use)], 1)

                def scores(j):
                    taken(USE_PROJ[j] + 2)
                    taken(USE_PROJ[j] + 3)
                    if j:
                        pe.wait_ge(scores_copied, i * (QUAD * NB4) + NB4 * j)
                    for g in range(G):
                        q, k = (qk_sb[:, j % 2, w, :, g * P:(g + 1) * P] for w in range(2))
                        last = parts3(score[:, g // 4, (g % 4) * P:(g % 4 + 1) * P], q, k)
                    last.then_inc(scores_ready, 1)

                def values(*gs):
                    if gs[0] == 0:
                        pe.wait_ge(split_ready, i * NSPLIT + SPLIT_ORDER.index(("v", 1)) + 1)
                    for g in gs:
                        use = USE_V[g]
                        dst = fill(use)
                        sum3(dst[:], [(x1_pair[:, :, k, g * P:(g + 1) * P], wv_pair[:, :, k]) for k in range(KB)]
                             ).then_inc(full[bank_of(use)], 1)

                def mix(j):
                    if j == 0:
                        for g in range(G - NBANK, G):
                            taken(USE_V[g])
                    pe.wait_ge(ptx_ready, i * (QUAD * NB4) + NB4 * (j + 1))
                    for h in range(NH):
                        use = USE_PV[j] + h
                        dst = fill(use)
                        for g in range(4 * h, 4 * h + 4):
                            last = parts3(dst[:, (g % 4) * P:(g % 4 + 1) * P], v_sb[:, g, :, j * DH:(j + 1) * DH],
                                          ptx[:, :, g])
                        last.then_inc(full[bank_of(use)], 1)

                def out_project(pair, c, js):
                    use = USE_OUT[pair][c]
                    h, ob = c // KB, c % KB
                    first, end = js[0] == 2 * pair, js[-1] == 2 * pair + 1
                    if c == 0:
                        for j in js:
                            taken(USE_PV[j])
                            taken(USE_PV[j] + 1)
                        if (pair, first) == (0, True):
                            pe.wait_ge(split_ready, i * NSPLIT + SPLIT_ORDER.index(("o", 1)) + 1)
                    dst = fill(use) if first else bank[bank_of(use)]
                    last = sum3(dst[:], [(wo_pair[:, :, j, ob * P:(ob + 1) * P], ao_pair[:, j, :, h * HALF:(h + 1) * HALF])
                                         for j in js], first, end)
                    if end:
                        last.then_inc(full[bank_of(use)], 1)

                project(0)
                values(0, 1)
                scores(0)
                values(2, 3, 4, 5)
                project(1)
                values(6, 7)
                scores(1)
                project(2)
                mix(0)
                scores(2)
                project(3)
                mix(1)
                scores(3)
                out_project(0, 0, [0, 1])
                out_project(0, 1, [0, 1])
                mix(2)
                out_project(0, 2, [0, 1])
                out_project(1, 0, [2])
                out_project(1, 1, [2])
                mix(3)
                out_project(0, 3, [0, 1])
                out_project(1, 0, [3])
                out_project(1, 1, [3])
                out_project(1, 2, [2, 3])
                out_project(1, 3, [2, 3])

            def fill(use):
                pe.wait_ge(free[bank_of(use)], count_of(use))
                return bank[bank_of(use)]

            def product(use, weights, rhs, nk):
                dst = fill(use)
                for k in range(nk):
                    last = mm(dst[:], weights(k), rhs(k), k == 0, k == nk - 1)
                last.then_inc(full[bank_of(use)], 1)

            for h in range(NH):
                pe.wait_ge(x2_ready, KB * (h + 1))
                mean_of(acc, NH + h)
            for h in range(NH):
                var_of(NH + h)
            pe.wait_ge(late_loaded, 9 * 16)
            def hidden_layer(h):
                pe.wait_ge(x1_ready, NH + h + 1)
                for m in range(MB):
                    product(USE_F1[h] + m, lambda k: f1_sb[:, k, m * P:(m + 1) * P],
                            lambda k: x1[:, k, h * HALF:(h + 1) * HALF], KB)

            def output_layer(h):
                for use in range(USE_F1[h] + MB - NBANK, USE_F1[h] + MB):
                    pe.wait_ge(free[bank_of(use)], count_of(use) + 1)
                for ob in range(KB):
                    product(USE_F2[h] + ob, lambda k: f2_sb[:, k, ob * P:(ob + 1) * P],
                            lambda k: hid[:, k, h * HALF:(h + 1) * HALF], MB)

            def gates(h):
                pe.wait_ge(x3_ready, (h + 1) * KB)
                for ob in range(KB):
                    for w, weights in enumerate((wz_sb, wn_sb)):
                        product(USE_GRU[h] + 2 * ob + w, lambda k: weights[:, k, ob * P:(ob + 1) * P],
                                lambda k: acc[:, k, h * HALF:(h + 1) * HALF], KB)

            hidden_layer(0)
            output_layer(0)
            hidden_layer(1)
            gates(0)
            output_layer(1)
            gates(1)

            def hidden(m, q):
                for k in range(KB):
                    last = mm(bank[m // 4][:, m % 4 * P:(m % 4 + 1) * P], w1_sb[:, k, m * P:(m + 1) * P], q[:, k],
                              k == 0, k == KB - 1)
                return last

            def logits(q):
                for k in range(KB):
                    last = mm(score[:, 1, 0:NBLK], q[:, k], wr_sb[:, k], k == 0, k == KB - 1)
                return last

            with pe.Fori(0, T // UNROLL) as i:
                for n in range(4 * UNROLL):
                    dst = score[:, 0]
                    pe.wait_ge(th16_ready, i * (4 * UNROLL) + n + 1)
                    first = True
                    for parts, src, ready in ((coup_parts, th16, None), (coup_parts[0:2], thlo, lo_ready)):
                        if ready is not None:
                            pe.wait_ge(ready, i * (4 * UNROLL) + n + 1)
                        for part in parts:
                            for ob in range(KB):
                                for k in range(KB):
                                    last = mm(dst[:, ob * B:(ob + 1) * B], part[:, k, ob * P:(ob + 1) * P],
                                              src[:, k * B:(k + 1) * B], first, False, skip_group_check=True)
                                    first = False
                    last.then_inc(coupled, 1)
                    m = n - FIRST_HIDDEN
                    if 0 <= m < MB:
                        hidden(m, q_group)
                    if m == MB:
                        logits(q_group)

            flat = trace.rearrange("p k t b -> p k (t b)")[:, :, B:]
            pe.wait_ge(trace_done, T + 1)
            logits(flat[:, :, N - P:]).then_inc(logits_ready, 1)
            for m in range(MB):
                last = hidden(m, flat[:, :, N - P:])
                if m % 4 == 3:
                    last.then_inc(hidden_ready, 1)
            def masks(h, m):
                n = h * MB + m
                places, groups = LAST[h]
                if m == 0:
                    pe.wait_ge(mask_ready, (h + 1) * len(groups))
                if n >= 3:
                    pe.wait_ge(h_ready, n - 2)
                for g in range(len(groups)):
                    last = mm(mask_bank(n)[:, g * P:(g + 1) * P], maskx[:, places.start + g, m * P:(m + 1) * P],
                              ident[:], True, True)
                last.then_inc(maskb_ready, 1)

            for m in range(3):
                masks(0, m)
            for h, (places, groups) in enumerate(LAST):
                dst = [fill(USE_G2[h] + ob) for ob in range(KB)]
                for k in range(MB):
                    pe.wait_ge(h_ready, h * MB + k + 1)
                    for ob in range(KB):
                        last = mm(dst[ob][:], w2_sb[:, k, ob * P:(ob + 1) * P], hid_of[:, places, k],
                                  k == 0, k == MB - 1)
                        if k == MB - 1:
                            last.then_inc(full[bank_of(USE_G2[h] + ob)], 1)
                    n = h * MB + k + 3
                    if n < NH * MB:
                        masks(n // MB, n % MB)

        @block.vector
        def _(dve):
            own = Own(dve, dve_step)
            V = nc.vector
            for b in range(NBANK):
                V.memset(sq[:, b:b + 1], 0.0).then_inc(free[b], 1)
            V.memset(eps[:], LN_EPS).then_inc(eps_ready, 1)
            own.step(V.memset(lg[:, :, NBLK:], BIG))

            def mod(c, k, h):
                nb = HALF // T
                return ada[:, c, k, h * nb:(h + 1) * nb].unsqueeze(2).broadcast_to([P, nb, T])

            def tok(ap):
                return ap.rearrange("p (b t) -> p b t", t=T)

            def centre(src, n):
                h = n % NH
                dve.wait_ge(mean_ready, n + 1)
                for k in range(KB):
                    V.tensor_tensor(centred_of[h][k], src[:, k, h * HALF:(h + 1) * HALF], score[:, h], ALU.subtract
                                    ).then_inc(centred_ready, 1)

            def normalised(n, dst):
                h = n % NH
                s = slice(h * HALF, (h + 1) * HALF)
                dve.wait_ge(rstd_ready, n + 1)
                own.step(V.tensor_tensor(newton, rstd[:, h], rstd[:, h], ALU.mult))
                own.wait()
                own.step(V.scalar_tensor_tensor(newton, newton, -0.5, var[:, h], ALU.mult, ALU.mult))
                own.wait()
                own.step(V.scalar_tensor_tensor(rstd[:, h], newton, 1.5, rstd[:, h], ALU.add, ALU.mult))
                own.wait()
                for k in range(KB):
                    own.step(V.tensor_tensor(dst[:, k, s], centred_of[h][k], rstd[:, h], ALU.mult))

            def modulate(n, shift, scale, dst, apart=False):
                h = n % NH
                s = slice(h * HALF, (h + 1) * HALF)
                own.wait()
                for k in range(KB):
                    own.step(V.tensor_tensor(tok(dst[:, k, s]), tok(dst[:, k, s]), mod(scale, k, h), ALU.mult))
                own.wait()
                for k in range(KB):
                    last = V.tensor_tensor(tok(dst[:, k, s]), tok(dst[:, k, s]), mod(shift, k, h), ALU.add)
                    if apart:
                        last.then_inc(normed, 1)
                    elif k < KB - 1:
                        own.step(last)
                if apart:
                    for k in range(KB):
                        dve.wait_ge(x1_high_ready, h * KB + k + 1)
                        last = V.tensor_tensor(x1_pair[:, 1, k, s], dst[:, k, s], x1_pair[:, 0, k, s], ALU.subtract)
                        if k < KB - 1:
                            own.step(last)
                last.then_inc(x1_ready, 1)

            for h in range(NH):
                dve.wait_ge(x_loaded[h], 16)
                centre(x_sb, h)
            dve.wait_ge(small_loaded, 48)
            for k in range(KB):
                own.step(V.tensor_copy(acc[:, k], v_("out_b", k).broadcast_to([P, N])))
            for h in range(NH):
                normalised(h, drive)
            dve.wait_ge(ada_summed, 1)
            own.step(V.tensor_tensor(
                ada[:].rearrange("p a k b -> p (a k) b"), bank[0][:, 0:12 * B].rearrange("p (a b) -> p a b", b=B),
                v_("ada_b").unsqueeze(2).broadcast_to([P, 12, B]), ALU.add))
            own.wait()
            for c in (SCALE1, SCALE2):
                own.step(V.tensor_scalar(ada[:, c], ada[:, c], 1.0, None, ALU.add))
            for h in range(NH):
                modulate(h, SHIFT1, SCALE1, drive, True)
            own.wait()

            STEPS = QUAD * 4
            PAIRS = 4 * QUAD + G + NH * QUAD
            start = own.n
            with dve.Fori(0, NQUAD) as i:
                own.n, own.base = 0, i * STEPS + start
                for w, name in enumerate(("q_b", "k_b", "v_b")):
                    V.tensor_scalar(pass_b[:, w], vec[:, bass.ds(i * QUAD + VEC[name][0], QUAD)], WSCALE, None,
                                    ALU.mult).then_inc(bias_ready, 1)
                dve.wait_ge(bias_ready, i * 3 + 3)
                pairs = [0]

                def low(use, hi, lo, bias=None):
                    pairs[0] += 1
                    dve.wait_ge(high_ready, i * PAIRS + pairs[0])
                    if bias is None:
                        ins = V.tensor_tensor(lo, bank[bank_of(use)][:], hi, ALU.subtract)
                    else:
                        ins = V.scalar_tensor_tensor(lo, bank[bank_of(use)][:], bias, hi, ALU.add, ALU.subtract)
                    ins.then_inc(free[bank_of(use)], 1)

                def low_proj(j, k):
                    h, w = k // 2, k % 2
                    hi, lo = (qk_sb[:, j % 2, w, c, h * HALF:(h + 1) * HALF] for c in range(2))
                    low(USE_PROJ[j] + k, hi, lo, pass_b[:, w, j:j + 1])

                def shift(j):
                    dve.wait_ge(scores_copied, i * (QUAD * NB4) + NB4 * (j + 1))
                    own.step(V.tensor_reduce(smax[:], sraw[:], AX_X, ALU.max))
                    own.wait()
                    V.tensor_tensor(sc[:], sraw[:], smax[:].unsqueeze(2).broadcast_to([P, G, T]), ALU.subtract
                                    ).then_inc(shifted, 1)

                def normalise(j):
                    dve.wait_ge(exp_ready, i * QUAD + j + 1)
                    own.step(V.tensor_reduce(ssum[:], pe_[:], AX_X, ALU.add))
                    own.wait()
                    own.step(V.reciprocal(srec[:], ssum[:]))
                    own.wait()
                    own.step(V.tensor_tensor(pn[:], pe_[:], srec[:].unsqueeze(2).broadcast_to([P, G, T]), ALU.mult))
                    own.wait()
                    if j:
                        dve.wait_ge(ptx_ready, i * (QUAD * NB4) + NB4 * j)
                    V.transpose(pt[:].rearrange("p g t -> p (g t)"), pn[:].rearrange("p g t -> p (g t)")
                                ).then_inc(pt_ready, 1)

                def low_projs(j):
                    for k in range(4):
                        low_proj(j, k)

                def low_values(*gs):
                    for g in gs:
                        low(USE_V[g], v_sb[:, g, 0], v_sb[:, g, 1])

                def low_pv(j):
                    for h in range(NH):
                        hi, lo = (ao_pair[:, j, c, h * HALF:(h + 1) * HALF] for c in range(2))
                        low(USE_PV[j] + h, hi, lo, pass_b[:, 2, j:j + 1])

                def add_heads(pair, c):
                    use = USE_OUT[pair][c]
                    a = acc[:, c % KB, c // KB * HALF:(c // KB + 1) * HALF]
                    dve.wait_ge(full[bank_of(use)], i * NPAR + count_of(use))
                    V.scalar_tensor_tensor(a, bank[bank_of(use)][:], WSCALE ** -2, a, ALU.mult, ALU.add
                                           ).then_inc(free[bank_of(use)], 1)

                low_projs(0)
                low_values(0, 1)
                shift(0)
                low_values(2)
                normalise(0)
                low_values(3, 4, 5)
                low_projs(1)
                low_values(6, 7)
                shift(1)
                normalise(1)
                low_projs(2)
                low_pv(0)
                shift(2)
                normalise(2)
                low_projs(3)
                low_pv(1)
                shift(3)
                add_heads(0, 0)
                normalise(3)
                add_heads(0, 1)
                low_pv(2)
                add_heads(0, 2)
                low_pv(3)
                add_heads(0, 3)
                for c in range(KB * NH):
                    add_heads(1, c)
                assert own.n == STEPS and pairs[0] == PAIRS
            own.n, own.base = start + NQUAD * STEPS, 0
            for use in range(AFTER - NBANK, AFTER):
                dve.wait_ge(free[bank_of(use)], count_of(use) + 1)

            for h in range(NH):
                s = slice(h * HALF, (h + 1) * HALF)
                for ob in range(KB):
                    own.step(V.tensor_tensor(tok(acc[:, ob, s]), tok(acc[:, ob, s]), mod(GATE1, ob, h), ALU.mult))
                own.wait()
                for ob in range(KB):
                    V.tensor_tensor(acc[:, ob, s], acc[:, ob, s], x_sb[:, ob, s], ALU.add).then_inc(x2_ready, 1)
            dve.wait_ge(x2_ready, KB * NH)
            for h in range(NH):
                centre(acc, NH + h)
            for h in range(NH):
                normalised(NH + h, x1)
                modulate(NH + h, SHIFT2, SCALE2, x1)

            dve.wait_ge(late_loaded, 9 * 16)
            own.step(V.tensor_copy(coup_parts[0][:], coup_sb[:]))
            own.wait()
            own.step(V.tensor_tensor(coup_rest[:], coup_sb[:], coup_parts[0][:], ALU.subtract))
            own.wait()
            own.step(V.tensor_copy(coup_parts[1][:], coup_rest[:]))
            own.wait()
            own.step(V.tensor_tensor(coup_parts[2][:], coup_rest[:], coup_parts[1][:], ALU.subtract))
            own.wait()
            V.tensor_scalar(hb[:], v_("bz"), 0.5, None, ALU.mult).then_inc(coup_ready, 1)

            def wait_full(use):
                dve.wait_ge(full[bank_of(use)], count_of(use))

            def residual(h):
                s = slice(h * HALF, (h + 1) * HALF)
                for ob in range(KB):
                    use = USE_F2[h] + ob
                    wait_full(use)
                    tmp = centred[:, ob]
                    own.step(V.tensor_scalar(tmp, bank[bank_of(use)][:], v_("ffn_b2", ob), None, ALU.add))
                    own.wait()
                    V.tensor_tensor(tok(tmp), tok(tmp), mod(GATE2, ob, h), ALU.mult).then_inc(free[bank_of(use)], 1)
                    dve.wait_ge(free[bank_of(use)], count_of(use) + 1)
                    V.tensor_tensor(acc[:, ob, s], acc[:, ob, s], tmp, ALU.add).then_inc(x3_ready, 1)

            def min_gru(h):
                s = slice(h * HALF, (h + 1) * HALF)
                for ob in range(KB):
                    n = h * KB + ob
                    use = USE_GRU[h] + 2 * ob
                    dve.wait_ge(free[bank_of(use)], count_of(use) + 1)
                    own.step(V.tensor_scalar(za[:], tz[:], -0.5, 0.5, ALU.mult, ALU.add))
                    own.step(V.tensor_scalar(zb, tz[:], 0.5, 0.5, ALU.mult, ALU.add))
                    dve.wait_ge(free[bank_of(use + 1)], count_of(use + 1) + 1)
                    V.tensor_scalar(nneg, nn_[:], 0.0, None, ALU.min).then_inc(gate_in, 1)
                    own.step(V.tensor_scalar(npos[:], nn_[:], 0.0, 0.5, ALU.max, ALU.add))
                    dve.wait_ge(tn_ready, n + 1)
                    own.wait()
                    own.step(V.scalar_tensor_tensor(npos[:], tn[:], 0.5, npos[:], ALU.mult, ALU.add))
                    own.wait()
                    own.step(V.tensor_tensor(zb, zb, npos[:], ALU.mult))
                    own.wait()
                    a0, b0 = tok(za[:])[:, :, 0:1], tok(zb)[:, :, 0:1]
                    own.step(V.scalar_tensor_tensor(b0, a0, 0.5, b0, ALU.mult, ALU.add))
                    own.wait()
                    own.step(V.memset(a0, 0.0))
                    own.wait()
                    own.step(V.tensor_tensor_scan(npos[:], za[:], zb, 0.0, ALU.mult, ALU.add))
                    own.wait()
                    V.tensor_tensor(drive[:, ob, s], x_sb[:, ob, s], npos[:], ALU.add).then_inc(z_used, 1)
                    dve.wait_ge(z_used, n + 1)

            for h in range(NH):
                residual(h)
                min_gru(h)
            for ob in range(KB):
                own.step(V.tensor_scalar(dbias[:, :, ob * B:(ob + 1) * B],
                                         drive[:, ob].rearrange("p (b t) -> p t b", t=T), v_("c2_b", ob), None, ALU.add))
            own.step(V.memset(padded[:, :, 0:UNROLL - 1], 0.0))
            V.tensor_copy(qp[:, 0, KB * B:], cond_sb[:].rearrange("p k b -> p (k b)")).then_inc(p_ready, 1)
            own.wait()
            V.tensor_copy(qn[:], cond_sb[:].rearrange("p k b -> p (k b)")).then_inc(q_ready, 1)
            dve.wait_ge(p_ready, 1)
            dve.wait_ge(q_ready, 1)

            H1, H2, H6 = STAGE_H[0], STAGE_H[2], STAGE_H[3]
            RK = 23
            start = own.n
            stt = V.scalar_tensor_tensor
            w64 = KB * B
            q_, p_ = (lambda s: qp[:, s, 0:w64]), (lambda s: qp[:, s, w64:])
            with dve.Fori(0, T // UNROLL) as i:
                own.n, own.base = 0, i * (UNROLL * RK) + start

                def mark(ins):
                    own.step(ins)
                    return own.n

                def wait_for(n):
                    dve.wait_ge(dve_step, own.base + n)

                for u in range(UNROLL):
                    t4, t3 = i * (4 * UNROLL) + 4 * u, i * (3 * UNROLL) + 3 * u
                    d_t = dbias[:, bass.ds(i * UNROLL + u, 1)].rearrange("p a c -> p (a c)")
                    V.tensor_scalar(q_(0), qn[:], CLAMP, -CLAMP, ALU.min, ALU.max).then_inc(clip_ready, 1)
                    dve.wait_ge(clip_ready, i * UNROLL + u + 1)
                    for s in range(4):
                        hs = STAGE_H[s]
                        if s == 1:
                            lined = mark(stt(lin[:, 1], p_(1), -H1, qd[:, 0], ALU.mult, ALU.add))
                        if s == 2:
                            lined = mark(stt(lin[:, 0], p_(2), -H2, qd[:, 1], ALU.mult, ALU.add))
                        if s == 3:
                            lined4 = mark(stt(lin4[:], comb[:], 1.0 / 3.0, d6[:], ALU.mult, ALU.add))
                        if s:
                            dve.wait_ge(q_ready, t4 + s + 1)
                        squared = mark(V.tensor_tensor(sq[:], q_(s), q_(s), ALU.mult))
                        if s == 0:
                            lined = mark(stt(qd[:, 0], d_t, H1, q_(0), ALU.mult, ALU.add))
                        if s in (1, 2):
                            dve.wait_ge(bp_ready, t3 + s + 1)
                            stt(p_(s + 1), q_(s), hs * EPSILON, bp[:], ALU.mult, ALU.add).then_inc(p_ready, 1)
                        if s == 3:
                            dve.wait_ge(pacc_ready, i * UNROLL + u + 1)
                            pended = mark(stt(pend[:], q_(3), H6 * EPSILON, pacc[:], ALU.mult, ALU.add))
                        dve.wait_ge(th32_ready, t4 + s + 1)
                        V.tensor_tensor(thlo[:], th32[:], th16[:], ALU.subtract).then_inc(lo_ready, 1)
                        wait_for(squared)
                        cubed = mark(stt(cub[:], sq[:], -3.0 if s < 3 else -3.0 - 1.0 / hs, q_(s), ALU.add, ALU.mult))
                        if s == 0:
                            wait_for(lined)
                            cubed = mark(stt(lin[:, 0], p_(0), -H1, qd[:, 0], ALU.mult, ALU.add))
                            dve.wait_ge(bp_ready, t3 + 1)
                            stt(p_(1), q_(0), hs * EPSILON, bp[:], ALU.mult, ALU.add).then_inc(p_ready, 1)
                        if s == 1:
                            mark(stt(qd[:, 1], d_t, H2, q_(0), ALU.mult, ALU.add))
                            differed = mark(V.tensor_tensor(comb[:], q_(1), q_(0), ALU.subtract))
                        if s == 2:
                            wait_for(differed)
                            mark(stt(comb[:], q_(2), 2.0, comb[:], ALU.mult, ALU.add))
                            mark(V.tensor_scalar(d6[:], d_t, H6, None, ALU.mult))
                        if s == 3:
                            wait_for(lined4)
                            cubed = mark(stt(lin[:, 1], p_(3), -H6, lin4[:], ALU.mult, ALU.add))
                            wait_for(pended)
                            V.tensor_scalar(p_(0), pend[:], CLAMP, -CLAMP, ALU.min, ALU.max).then_inc(p_ready, 1)
                        wait_for(cubed)
                        based = mark(stt(base[:], cub[:], -hs / 3.0, lin[:, s % 2], ALU.mult, ALU.add))
                        dve.wait_ge(p_ready, t4 + s + 2)
                        wait_for(based)
                        dve.wait_ge(coupled, t4 + s + 1)
                        stt(q_(s + 1) if s < 3 else qn[:], score[:, 0, 0:w64], hs, base[:], ALU.mult, ALU.add
                            ).then_inc(q_ready, 1)
                    dve.wait_ge(q_ready, t4 + 5)
                assert own.n == RK * UNROLL, own.n
            own.n, own.base = start + T * RK, 0
            V.tensor_scalar(trace[:, :, T], qn[:].rearrange("p (k b) -> p k b", k=KB), CLAMP, -CLAMP, ALU.min,
                            ALU.max).then_inc(trace_done, 1)

            dve.wait_ge(logits_ready, 1)
            own.step(V.tensor_copy(lg[:, 0, 0:NBLK], score[:, 1, 0:NBLK]))
            own.wait()
            own.step(V.tensor_tensor(lg[:, :, 0:NBLK], lg[:, :, 0:NBLK],
                                     br_sb[:].unsqueeze(1).broadcast_to([P, G, NBLK]), ALU.add))
            own.wait()
            for g in range(G):
                own.step(V.max(top8[:, g], lg[:, g]))
            own.wait()
            for g in range(G):
                own.step(V.match_replace(lgr[:, g], top8[:, g], lg[:, g], -BIG))
            own.wait()
            own.step(V.tensor_scalar(mask[:], lgr[:, :, 0:NBLK], -BIG, None, ALU.is_equal))
            own.wait()
            def expand(places):
                for g in range(places.start, places.stop):
                    V.tensor_copy(maskx[:, g].rearrange("p (c r) -> p c r", c=NBLK),
                                  mask[:, g].unsqueeze(2).broadcast_to([P, NBLK, MLP // NBLK])).then_inc(mask_ready, 1)

            n = 0
            for h, (places, groups) in enumerate(LAST):
                expand(places)
                if G - 1 in groups:
                    dve.wait_ge(gelu_ready, 2)
                for m in range(MB):
                    dve.wait_ge(maskb_ready, n + 1)
                    V.tensor_tensor(hid_of[:, places, m], hid_of[:, places, m],
                                    mask_bank(n).rearrange("p (g n) -> p g n", n=P), ALU.mult).then_inc(h_ready, 1)
                    n += 1
            for h, (places, groups) in enumerate(LAST):
                for ob in range(KB):
                    use = USE_G2[h] + ob
                    wait_full(use)
                    at = 0
                    for a, b in runs(groups):
                        V.tensor_tensor(osb[:, ob, a * P:b * P].rearrange("p (t b) -> p t b", b=B),
                                        bank[bank_of(use)][:, at * P:(at + b - a) * P].rearrange(
                                            "p (t b) -> p t b", b=B),
                                        drive[:, ob].rearrange("p (b t) -> p t b", t=T)[:, a * UNROLL:b * UNROLL],
                                        ALU.add).then_inc(out_ready, 1)
                        at += b - a


def kernel(**inputs):
    import numpy as np
    import concourse.bacc as bacc
    from concourse.bass_utils import run_bass_kernel_spmd

    a = {k: np.asarray(v) for k, v in inputs.items()}

    def rows(w, *shape):
        return w.reshape(-1, P, *w.shape[1:]).swapaxes(0, 1).reshape(P, -1, *(shape or w.shape[1:]))

    def column(v):
        return v.reshape(-1, P).T

    qkv = a["L0_cond_qkv_w"].reshape(KB, P, 3, H, DH)
    arrays = {
        "xT": rows(a["x"].transpose(2, 0, 1).reshape(D, N)),
        "condT": rows(a["cond_2048"].T),
        "ada_w": rows(a["L0_cond_ada_w"]),
        "vecs": np.concatenate([column(v) for v in (
            a["L0_cond_ada_b"], *a["L0_cond_qkv_b"].reshape(3, -1), a["L0_cond_out_b"], a["L0_cond_ffn_b1"],
            a["L0_cond_ffn_b2"], a["L0_attn_bz"], a["L0_attn_bn"], a["L0_cond2_bias"])], axis=1),
        "br": np.repeat(a["L0_ffn_br"][None], P, axis=0),
        "wqk": qkv[:, :, 0:2].transpose(3, 1, 0, 2, 4),
        "wv": qkv[:, :, 2].reshape(KB, P, NQUAD, QUAD * DH).transpose(2, 1, 0, 3),
        "wo": a["L0_cond_out_w"].reshape(H, DH, D).transpose(1, 0, 2),
        "ffn_w1": rows(a["L0_cond_ffn_w1"]),
        "ffn_w2": rows(a["L0_cond_ffn_w2"]),
        "wzT": rows(a["L0_attn_Wz"].T),
        "wnT": rows(a["L0_attn_Wn"].T),
        "coupT": rows(a["L0_cond2_coupling"].T),
        "wrT": rows(a["L0_ffn_Wr"].T),
        "w1T": rows(a["L0_ffn_W1"].T),
        "w2T": rows(a["L0_ffn_W2"].T),
    }
    arrays = {k: np.ascontiguousarray(v) for k, v in arrays.items()}
    nc = bacc.Bacc("TRN2", target_bir_lowering=False, num_devices=1)
    args = [nc.dram_tensor(k, v.shape, mybir.dt.from_np(v.dtype), kind="ExternalInput").ap() for k, v in arrays.items()]
    out = nc.dram_tensor("out_0_dram", (P, KB, N), F32, kind="ExternalOutput").ap()
    build(nc, *args, out)
    r = run_bass_kernel_spmd(nc, [arrays], core_ids=[0])
    got = r.results[0]["out_0_dram"].reshape(P, KB, T, B)
    return np.ascontiguousarray(got.transpose(3, 2, 1, 0).reshape(B, T, D))
```

```python
from contextlib import ExitStack

import concourse.bass as bass
from concourse import mybir

ALU = mybir.AluOpType
ACT = mybir.ActivationFunctionType
F32 = mybir.dt.float32
F16 = mybir.dt.float16
BF16 = mybir.dt.bfloat16
AX_X = mybir.AxisListType.X

P = 128
B, T, D = 32, 32, 256
N = B * T
KB = D // P
H, DH = 16, 128
QUAD = 4
NQUAD = H // QUAD
HALF = N // 2
NH = N // HALF
G = N // P
NB4 = P // T
MLP = 4 * D
MB = MLP // P
NBLK, TOPK = 16, 4
LN_EPS = 1e-6
SCALE = float(DH) ** -0.5
DT, EPSILON, ALPHA, BETA, CLAMP = 0.01, 0.08, 0.7, 0.8, 20.0
UNROLL = 4
STAGE_H = (0.5 * DT, 0.5 * DT, DT, DT / 6.0)
BIG = 3.0e38

VEC = {}
_at = 0
for _name, _n in (("ada_b", 12), ("q_b", H), ("k_b", H), ("v_b", H), ("out_b", KB), ("ffn_b1", MB), ("ffn_b2", KB),
                  ("bz", KB), ("bn", KB), ("c2_b", KB)):
    VEC[_name] = (_at, _at + _n)
    _at += _n
NVEC = _at

SHIFT1, SCALE1, GATE1, SHIFT2, SCALE2, GATE2 = range(6)

NBANK = 5
USE_PROJ = [0, 10, 16, 22]
USE_V = [4, 5, 6, 7, 8, 9, 14, 15]
USE_PV = [20, 26, 30, 35]
USE_OUT = [[28, 29, 32, 37], [33, 34, 38, 39]]
USES_PER_PASS = 40
CSCALE = 64.0
SPLIT_ORDER = [("qk", 0), ("v", 0), ("v", 1), ("qk", 1), ("qk", 2), ("o", 0), ("o", 1), ("qk", 3)]
WSCALE = 16.0


def build(nc, xT, condT, ada_w, vecs, br, wqk, wv, wo, ffn_w1, ffn_w2, wzT, wnT, coupT, wrT, w1T, w2T, out):
    with ExitStack() as ctx:
        def sb(name, shape, dt=F32):
            return ctx.enter_context(nc.sbuf_tensor(name, shape, dt))

        def sem(name):
            return ctx.enter_context(nc.semaphore(name))

        bank = [ctx.enter_context(nc.psum_tensor(f"bank{i}", [P, 512], F32)) for i in range(NBANK)]
        score = ctx.enter_context(nc.psum_tensor("score", [P, 2, 512], F32))
        spare = ctx.enter_context(nc.psum_tensor("spare", [P, 512], F32))

        x_sb = sb("x_sb", [P, KB, N])
        cond_sb = sb("cond_sb", [P, KB, B])
        adaw_sb = sb("adaw_sb", [P, KB, 6 * D])
        vec = sb("vec", [P, NVEC])
        br_sb = sb("br_sb", [P, NBLK])
        wqk_sb = sb("wqk_sb", [P, QUAD, KB, 2, DH])
        wv_sb = sb("wv_sb", [P, KB, QUAD * DH])
        wo_sb = sb("wo_sb", [P, QUAD, D])
        f1_sb = sb("f1_sb", [P, KB, MLP])
        f2_sb = sb("f2_sb", [P, MB, D])
        wz_sb = sb("wz_sb", [P, KB, D])
        wn_sb = sb("wn_sb", [P, KB, D])
        coup_sb = sb("coup_sb", [P, KB, D])
        coup_rest = sb("coup_rest", [P, KB, D])
        coup_parts = [sb(f"coup_part{i}", [P, KB, D], F16) for i in range(2)]
        wr_sb = sb("wr_sb", [P, KB, NBLK])
        w1_sb = sb("w1_sb", [P, KB, MLP])
        w2_sb = sb("w2_sb", [P, MB, D])

        ones = sb("ones", [P, P])
        ident = sb("ident", [P, P], BF16)

        ada = sb("ada", [P, 6, KB, B])
        centred = sb("centred", [P, KB, HALF])
        square = sb("square", [P, KB, HALF])
        var = sb("var", [P, NH, HALF])
        newton = coup_rest[:].rearrange("p k n -> p (k n)")
        rstd = sb("rstd", [P, NH, HALF])
        eps = sb("eps", [P, 1])
        eps_log = sb("eps_log", [P, 1])
        x1 = sb("x1", [P, KB, N])

        big = sb("big", [P, 2 * 4096])
        qk_sb = big[:, 0:4096].bitcast(F16).rearrange("p (r w c n) -> p r w c n", r=2, w=2, c=2)
        v_sb = big[:, 4096:8192].bitcast(F16).rearrange("p (g c n) -> p g c n", g=G, c=2)
        hid = big[:, :].rearrange("p (m n) -> p m n", m=MB)
        hid_of = big[:, :].rearrange("p (s m n) -> p s m n", s=G, m=MB)
        ao_sb = sb("ao_sb", [P, QUAD, N])
        ao_pair = ao_sb[:].rearrange("p j n -> p (j n)").bitcast(F16).rearrange("p (j c n) -> p j c n", j=QUAD, c=2)
        x1_pair = x1[:].rearrange("p k n -> p (k n)").bitcast(F16).rearrange("p (c k n) -> p c k n", c=2, k=KB)
        pairs_sb = adaw_sb[:].rearrange("p k n -> p (k n)").bitcast(F16)
        wqk_pair = pairs_sb[:, 0:2048].rearrange("p (r c n) -> p r c n", r=2, c=2)
        wv_pair = pairs_sb[:, 2048:4096].rearrange("p (c k n) -> p c k n", c=2, k=KB)
        wo_pair = pairs_sb[:, 4096:6144].rearrange("p (c j n) -> p c j n", c=2, j=QUAD)
        pass_b = sb("pass_b", [P, 3, QUAD])
        smax = sb("smax", [P, G])
        ssum = sb("ssum", [P, G])
        srec = sb("srec", [P, G])
        sc = sb("sc", [P, G, T])
        pe_ = sb("pe_", [P, G, T])
        pn = sb("pn", [P, G, T])
        pt = sb("pt", [P, G, T])
        sraw = sb("sraw", [P, G, T])
        ptx = sb("ptx", [P, 2, G, P], F16)
        acc = sb("acc", [P, KB, N])

        hb = sb("hb", [P, KB])
        nn_ = sb("nn_", [P, HALF])
        tz = sb("tz", [P, HALF])
        tz_of = (tz[:], var[:, 0])
        nn_of = (nn_[:], var[:, 1])
        wscale = tz
        nneg = square[:, 0]
        tn = sb("tn", [P, HALF])
        npos = sb("npos", [P, HALF])
        za = sb("za", [P, HALF])
        zb = square[:, 1]
        f1_pair = wqk_sb[:].rearrange("p j k w d -> p (j k w d)").bitcast(F16).rearrange("p (c n) -> p c n", c=2)
        f2_parts = (wv_sb[:].rearrange("p k n -> p (k n)").bitcast(F16), wo_sb[:].rearrange("p j n -> p (j n)").bitcast(F16))
        w2_pair = f1_sb[:].rearrange("p k n -> p (k n)").bitcast(F16).rearrange("p (c n) -> p c n", c=2)
        masked_pair = big[:, :].bitcast(F16).rearrange("p (s m c n) -> p s m c n", s=G, m=MB, c=2)
        hid_pair = big[:, :].bitcast(F16).rearrange("p (m c n) -> p m c n", m=MB, c=2)
        gelu_of = (npos[:], za[:])
        centred_of = ((centred[:, 0], centred[:, 1]), (nn_[:], tn[:]))
        square_of = ((square[:, 0], square[:, 1]), (npos[:], za[:]))
        drive = sb("drive", [P, KB, N])
        dbias = sb("dbias", [P, T, KB * B])

        qp = sb("qp", [P, 4, 2 * KB * B])
        padded = adaw_sb[:].rearrange("p k n -> p (k n)")[:, 0:KB * (T + UNROLL) * B].rearrange(
            "p (k t b) -> p k t b", k=KB, t=T + UNROLL)
        trace = padded[:, :, UNROLL - 1:]
        q_group = centred[:, 0, 0:KB * P].rearrange("p (k n) -> p k n", k=KB)
        th16 = sb("th16", [P, KB * B], F16)
        th32 = sb("th32", [P, KB * B])
        thlo = sb("thlo", [P, KB * B], F16)
        sq = sb("sq", [P, KB * B])
        cub = sb("cub", [P, KB * B])
        base = sb("base", [P, KB * B])
        qd = sb("qd", [P, 2, KB * B])
        pc = sb("pc", [P, 3, KB * B])
        pfac = sb("pfac", [P, 6, KB * B])
        pterm = sb("pterm", [P, 2, KB * B])
        bp = sb("bp", [P, KB * B])
        lin = sb("lin", [P, 2, KB * B])
        lin4 = sb("lin4", [P, KB * B])
        d6 = sb("d6", [P, KB * B])
        comb = sb("comb", [P, KB * B])
        pacc = sb("pacc", [P, KB * B])
        pend = sb("pend", [P, KB * B])
        qn = sb("qn", [P, KB * B])

        lg = sb("lg", [P, G, NBLK + TOPK])
        top8 = sb("top8", [P, G, 8])
        lgr = sb("lgr", [P, G, NBLK + TOPK])
        mask = sb("mask", [P, G, NBLK], BF16)
        maskx = ao_sb[:].rearrange("p j n -> p (j n)").bitcast(BF16).rearrange("p (g n) -> p g n", g=G)
        osb = x1

        def v_(name, j=None):
            a, b = VEC[name]
            return vec[:, a:b] if j is None else vec[:, a + j:a + j + 1]

        x_loaded = [sem(f"x_loaded{h}") for h in range(NH)]
        small_loaded = sem("small_loaded")
        late_loaded = sem("late_loaded")
        qk_loaded = [sem(f"qk_loaded{j}") for j in range(QUAD)]
        v_loaded = sem("v_loaded")
        o_loaded = sem("o_loaded")
        ones_ready = sem("ones_ready")
        ident_ready = sem("ident_ready")
        ada_summed = sem("ada_summed")
        mean_ready = sem("mean_ready")
        var_ready = sem("var_ready")
        centred_ready = sem("centred_ready")
        square_ready = sem("square_ready")
        rstd_ready = sem("rstd_ready")
        x1_ready = sem("x1_ready")
        dve_step = sem("dve_step")
        pool_step = sem("pool_step")
        act_step = sem("act_step")
        full = [sem(f"full{i}") for i in range(NBANK)]
        free = [sem(f"free{i}") for i in range(NBANK)]
        bias_ready = sem("bias_ready")
        scores_ready = sem("scores_ready")
        high_ready = sem("high_ready")
        shifted = sem("shifted")
        exp_ready = sem("exp_ready")
        pt_ready = sem("pt_ready")
        ptx_cleared = sem("ptx_cleared")
        scores_copied = sem("scores_copied")
        high_placed = sem("high_placed")
        ptx_ready = sem("ptx_ready")
        eps_ready = sem("eps_ready")
        normed = sem("normed")
        x1_high_ready = sem("x1_high_ready")
        scaled_ready = sem("scaled_ready")
        w_high_ready = sem("w_high_ready")
        split_ready = sem("split_ready")
        x2_ready = sem("x2_ready")
        mlp_scaled = sem("mlp_scaled")
        mlp_high_ready = sem("mlp_high_ready")
        mlp_split = sem("mlp_split")
        hid_high_ready = sem("hid_high_ready")
        hid_low_ready = sem("hid_low_ready")
        coup_ready = sem("coup_ready")
        x3_ready = sem("x3_ready")
        gate_in = sem("gate_in")
        z_used = sem("z_used")
        dbias_ready = sem("dbias_ready")
        tn_ready = sem("tn_ready")
        q_ready = sem("q_ready")
        clip_ready = sem("clip_ready")
        pacc_ready = sem("pacc_ready")
        trace_done = sem("trace_done")
        th16_ready = sem("th16_ready")
        th32_ready = sem("th32_ready")
        lo_ready = sem("lo_ready")
        coupled = sem("coupled")
        p_ready = sem("p_ready")
        bp_ready = sem("bp_ready")
        logits_ready = sem("logits_ready")
        chosen = sem("chosen")
        mask_ready = sem("mask_ready")
        act_mask_ready = sem("act_mask_ready")
        maskb_ready = sem("maskb_ready")
        hidden_ready = sem("hidden_ready")
        masked = sem("masked")
        masked_high_ready = sem("masked_high_ready")
        gelu_ready = sem("gelu_ready")
        h_ready = sem("h_ready")
        out_ready = sem("out_ready")
        stored = sem("stored")

        AFTER = NQUAD * USES_PER_PASS
        USE_F1 = [AFTER, AFTER + MB + KB]
        USE_GRU = [AFTER + 2 * MB + KB, AFTER + 2 * (MB + KB) + 2 * KB]
        USE_F2 = [AFTER + MB, AFTER + 2 * MB + KB + 2 * KB]
        USE_G2 = [AFTER + 2 * (MB + KB) + 2 * KB * NH + KB * h for h in range(NH)]
        LAST = [(slice(G // 2, G), list(range(G // 2 - 1, G - 1))), (slice(0, G // 2), [G - 1, *range(G // 2 - 1)])]
        FIRST_HIDDEN = 4
        GELU_AT = (9, 13)
        LOGITS_AT = 14

        def bank_of(use):
            return use % NBANK

        def count_of(use, start=0):
            return start * (USES_PER_PASS // NBANK) + use // NBANK + 1

        NPAR = USES_PER_PASS // NBANK
        NSPLIT = len(SPLIT_ORDER)

        def split_arrays(kind, part):
            if kind == "qk":
                return wqk_sb[:, part].rearrange("p k w d -> p (k w d)"), wqk_pair[:, part % 2]
            if kind == "v":
                return wv_sb[:, part], wv_pair[:, :, part]
            o = slice(part * QUAD // 2, (part + 1) * QUAD // 2)
            return wo_sb[:, o].rearrange("p j n -> p (j n)"), wo_pair[:, :, o].rearrange("p c j n -> p c (j n)")

        def mlp_arrays(t):
            f, t = t // 4, t % 4
            s = slice(t * 512, (t + 1) * 512)
            w = (f1_sb[:].rearrange("p k n -> p (k n)"), f2_sb[:].rearrange("p m n -> p (m n)"),
                 w2_sb[:].rearrange("p m n -> p (m n)"))[f][:, s]
            hi, lo = ((f1_pair[:, 0], f1_pair[:, 1]), f2_parts, (w2_pair[:, 0], w2_pair[:, 1]))[f]
            return w, hi[:, s], lo[:, s]

        class Own:

            def __init__(self, eng, semaphore):
                self.eng, self.sem, self.n, self.base = eng, semaphore, 0, 0

            def step(self, ins):
                ins.then_inc(self.sem, 1)
                self.n += 1

            def wait(self):
                self.eng.wait_ge(self.sem, self.base + self.n)

        def runs(groups):
            out_runs, first = [], 0
            for n in range(1, len(groups) + 1):
                if n == len(groups) or groups[n] != groups[n - 1] + 1:
                    out_runs.append((groups[first], groups[n - 1] + 1))
                    first = n
            return out_runs

        def var_bank(n):
            return spare[:] if n % NH == 0 else score[:, 0]

        DVE_EXPANDS, ACT_EXPANDS, ACT_EXPANDS_LATE = (4, 5), (6, 7), {1: 0, 3: 1, 4: 2, 5: 3}

        def mask_of(g):
            return (maskx[:, g].rearrange("p (c r) -> p c r", c=NBLK),
                    mask[:, g].unsqueeze(2).broadcast_to([P, NBLK, MLP // NBLK]))

        def mask_bank(n):
            return (spare[:], score[:, 0], score[:, 1])[n % 3]

        s8 = score[:].rearrange("p a (g s) -> p (a g) s", g=4)
        block = ctx.enter_context(nc.Block())

        @block.sync
        def _(sp):
            for h in range(NH):
                s = slice(h * HALF, (h + 1) * HALF)
                sp.dma_start(x_sb[:, :, s], xT[:, :, s]).then_inc(x_loaded[h], 16)
            for j in range(QUAD):
                sp.dma_start(wqk_sb[:, j], wqk[j]).then_inc(qk_loaded[j], 16)
            sp.dma_start(wv_sb[:], wv[0]).then_inc(v_loaded, 16)
            sp.dma_start(wo_sb[:], wo[:, 0:QUAD]).then_inc(o_loaded, 16)
            for dst, src in ((br_sb, br), (f1_sb, ffn_w1), (f2_sb, ffn_w2), (wz_sb, wzT), (wn_sb, wnT),
                             (coup_sb, coupT), (wr_sb, wrT), (w1_sb, w1T), (w2_sb, w2T)):
                sp.dma_start(dst[:], src).then_inc(late_loaded, 16)
            with sp.Fori(0, NQUAD - 1) as i:
                for t, (kind, part) in enumerate(SPLIT_ORDER):
                    if (kind, part) in (("v", 0), ("o", 0)):
                        continue
                    sp.wait_ge(split_ready, i * NSPLIT + t + 1)
                    if kind == "qk":
                        sp.dma_start(wqk_sb[:, part],
                                     wqk[bass.ds(i * QUAD + QUAD + part, 1)].rearrange("a p k w d -> (a p) k w d")
                                     ).then_inc(qk_loaded[part], 16)
                    elif kind == "v":
                        sp.dma_start(wv_sb[:], wv[bass.ds(i + 1, 1)].rearrange("a p k n -> (a p) k n")
                                     ).then_inc(v_loaded, 16)
                    else:
                        sp.dma_start(wo_sb[:], wo[:, bass.ds(i * QUAD + QUAD, QUAD)]).then_inc(o_loaded, 16)
            n = 0
            for _, groups in LAST:
                for ob in range(KB):
                    for a, b in runs(groups):
                        n += 1
                        sp.wait_ge(out_ready, n)
                        sp.dma_start(out[:, ob, a * P:b * P], osb[:, ob, a * P:b * P]).then_inc(stored, 16)
            sp.wait_ge(stored, 16 * n)

        @block.gpsimd
        def _(pool):
            own = Own(pool, pool_step)
            nc.gpsimd.memset(ones[:], 1.0 / D).then_inc(ones_ready, 1)
            own.step(nc.gpsimd.memset(ident[:], 0.0))
            own.wait()
            nc.gpsimd.affine_select(out=ident[:], in_=ident[:], compare_op=ALU.not_equal, fill=1.0, base=0,
                                    pattern=[[-1, P]], channel_multiplier=1).then_inc(ident_ready, 1)
            own.step(nc.gpsimd.memset(ptx[:], 0.0))
            own.step(nc.gpsimd.memset(wscale[:], WSCALE))
            for s, f in enumerate((*(-BETA * h * EPSILON for h in STAGE_H[0:3]), 2.0,
                                   1.0 - 3.0 * BETA * STAGE_H[3] * EPSILON, 1.0 / 3.0)):
                own.step(nc.gpsimd.memset(pfac[:, s], f))

            own.wait()
            nc.gpsimd.drain().then_inc(ptx_cleared, 1)
            with pool.Fori(0, NQUAD) as i:
                def scale(t):
                    kind, part = SPLIT_ORDER[t]
                    loaded = {"qk": qk_loaded[part % QUAD], "v": v_loaded, "o": o_loaded}[kind]
                    w, _ = split_arrays(kind, part)
                    pool.wait_ge(loaded, i * 16 + 16)
                    nc.gpsimd.tensor_tensor(w, w, wscale[:], ALU.mult).then_inc(scaled_ready, 1)

                def split(t):
                    w, pair = split_arrays(*SPLIT_ORDER[t])
                    pool.wait_ge(w_high_ready, i * NSPLIT + t + 1)
                    nc.gpsimd.tensor_tensor(pair[:, 1], w, pair[:, 0], ALU.subtract).then_inc(split_ready, 1)

                def place_low(j):
                    for q in range(NB4):
                        s = slice(q * T, (q + 1) * T)
                        pool.wait_ge(high_placed, i * (QUAD * NB4) + NB4 * j + q + 1)
                        nc.gpsimd.tensor_tensor(ptx[s, 1, :, s], pt[s], ptx[s, 0, :, s], ALU.subtract
                                                ).then_inc(ptx_ready, 1)

                scale(0)
                for t in range(NSPLIT):
                    if t + 1 < NSPLIT:
                        scale(t + 1)
                    split(t)
                    if t == 3:
                        pool.wait_ge(split_ready, i * NSPLIT + t + 1)
                        place_low(0)
                        pool.wait_ge(ptx_ready, i * (QUAD * NB4) + NB4)
                pool.wait_ge(split_ready, i * NSPLIT + NSPLIT)
                for j in range(1, QUAD):
                    place_low(j)
                pool.wait_ge(ptx_ready, i * (QUAD * NB4) + QUAD * NB4)
            pool.wait_ge(late_loaded, 9 * 16)
            for parts in (range(0, 8), range(8, 12)):
                for t in parts:
                    w, _, _ = mlp_arrays(t)
                    nc.gpsimd.tensor_tensor(w, w, wscale[:], ALU.mult).then_inc(mlp_scaled, 1)
                for t in parts:
                    w, high_part, low_part = mlp_arrays(t)
                    pool.wait_ge(mlp_high_ready, t + 1)
                    nc.gpsimd.tensor_tensor(low_part, w, high_part, ALU.subtract).then_inc(mlp_split, 1)
            pool.wait_ge(mlp_split, 12)
            pool.wait_ge(ptx_ready, NQUAD * QUAD * NB4)
            start = own.n
            gt = nc.gpsimd.tensor_tensor
            with pool.Fori(0, T // UNROLL) as i:
                own.n, own.base = 0, i * (11 * UNROLL) + start

                def p_(s):
                    return qp[:, s, KB * B:]

                for u, s in ((u, s) for u in range(UNROLL) for s in range(4)):
                    pool.wait_ge(p_ready, i * (4 * UNROLL) + 4 * u + s + 1)
                    if s < 3:
                        own.step(gt(bp[:], p_(s), pfac[:, s], ALU.mult))
                        if s == 0:
                            own.step(nc.gpsimd.tensor_scalar(pc[:, 0], p_(0), STAGE_H[0] * EPSILON * ALPHA, None, ALU.add))
                        own.wait()
                        gt(bp[:], bp[:], pc[:, s // 2], ALU.add).then_inc(bp_ready, 1)
                    if s == 0:
                        own.step(nc.gpsimd.tensor_scalar(pc[:, 1], p_(0), STAGE_H[2] * EPSILON * ALPHA, None, ALU.add))
                        own.step(nc.gpsimd.tensor_scalar(pc[:, 2], p_(0), -3.0 * STAGE_H[3] * EPSILON * ALPHA, None,
                                                         ALU.add))
                    if s == 1:
                        own.step(gt(pacc[:], p_(1), pc[:, 2], ALU.subtract))
                    if s >= 2:
                        own.step(gt(pterm[:, s - 2], p_(s), pfac[:, s + 1], ALU.mult))
                        own.wait()
                        own.step(gt(pacc[:], pacc[:], pterm[:, s - 2], ALU.add))
                    if s == 3:
                        own.wait()
                        gt(pacc[:], pacc[:], pfac[:, 5], ALU.mult).then_inc(pacc_ready, 1)
                assert own.n == 11 * UNROLL, own.n

        @block.scalar
        def _(act):
            own = Own(act, act_step)
            act.dma_start(cond_sb[:], condT).then_inc(small_loaded, 16)
            act.dma_start(adaw_sb[:], ada_w).then_inc(small_loaded, 16)
            act.dma_start(vec[:], vecs).then_inc(small_loaded, 16)

            def squares(n):
                for k in range(KB):
                    act.wait_ge(centred_ready, n * KB + k + 1)
                    nc.scalar.activation(square_of[n % NH][k], centred_of[n % NH][k], ACT.Square).then_inc(square_ready, 1)

            def log_table():
                nc.scalar.activation(eps_log[:], eps[:], ACT.Ln)

            def logs(n):
                h = n % NH
                act.wait_ge(var_ready, n + 1)
                own.step(nc.scalar.activation(rstd[:, h], var_bank(n), ACT.Ln, bias=eps[:]))
                own.step(nc.scalar.activation(var[:, h], var_bank(n), ACT.Identity, bias=eps[:]))

            def roots(n):
                nc.scalar.activation(rstd[:, n % NH], rstd[:, n % NH], ACT.Exp, scale=-0.5).then_inc(rstd_ready, 1)

            def x1_high(n):
                h = n % NH
                for k in range(KB):
                    s = slice(h * HALF, (h + 1) * HALF)
                    act.wait_ge(normed, n * KB + k + 1)
                    nc.scalar.activation(x1_pair[:, 0, k, s], drive[:, k, s], ACT.Copy).then_inc(x1_high_ready, 1)

            act.wait_ge(eps_ready, 1)
            for h in range(NH):
                squares(h)
            for h in range(NH):
                logs(h)
            own.wait()
            for h in range(NH):
                roots(h)
            for h in range(NH):
                x1_high(h)

            act.wait_ge(ptx_cleared, 1)
            with act.Fori(0, NQUAD) as i:
                def high(use, dst, bias=None):
                    act.wait_ge(full[bank_of(use)], i * NPAR + count_of(use))
                    src = bank[bank_of(use)][:]
                    if bias is None:
                        ins = nc.scalar.activation(dst, src, ACT.Copy)
                    else:
                        ins = nc.scalar.activation(dst, src, ACT.Identity, bias=bias)
                    ins.then_inc(high_ready, 1)

                def head_bias(name, j):
                    return pass_b[:, ("q_b", "k_b", "v_b").index(name), j:j + 1]

                def empty_proj(j, k):
                    h, w = k // 2, k % 2
                    high(USE_PROJ[j] + k, qk_sb[:, j % 2, w, 0, h * HALF:(h + 1) * HALF],
                         head_bias(("q_b", "k_b")[w], j))

                def empty_pv(j):
                    for h in range(NH):
                        high(USE_PV[j] + h, ao_pair[:, j, 0, h * HALF:(h + 1) * HALF], head_bias("v_b", j))

                def weights_high(t):
                    w, pair = split_arrays(*SPLIT_ORDER[t])
                    act.wait_ge(scaled_ready, i * NSPLIT + t + 1)
                    nc.scalar.activation(pair[:, 0], w, ACT.Copy).then_inc(w_high_ready, 1)

                def exps(j):
                    act.wait_ge(shifted, i * QUAD + j + 1)
                    nc.scalar.activation(pe_[:], sc[:], ACT.Exp, scale=SCALE / WSCALE ** 2).then_inc(exp_ready, 1)

                def copy_scores(j):
                    act.wait_ge(scores_ready, i * QUAD + j + 1)
                    for q in range(NB4):
                        s = slice(q * T, (q + 1) * T)
                        nc.scalar.activation(sraw[s], s8[s, :, s], ACT.Copy).then_inc(scores_copied, 1)

                def place_high(j):
                    act.wait_ge(pt_ready, i * QUAD + j + 1)
                    for q in range(NB4):
                        s = slice(q * T, (q + 1) * T)
                        nc.scalar.activation(ptx[s, 0, :, s], pt[s], ACT.Copy).then_inc(high_placed, 1)

                def empty_projs(j, ks=range(4)):
                    for k in ks:
                        empty_proj(j, k)

                def empty_values(*gs):
                    for g in gs:
                        high(USE_V[g], v_sb[:, g, 0])

                for t in range(4):
                    weights_high(t)
                act.wait_ge(bias_ready, i * 3 + 3)
                empty_projs(0)
                empty_values(0, 1)
                copy_scores(0)
                empty_values(2)
                exps(0)
                empty_values(3, 4)
                place_high(0)
                weights_high(4)
                empty_values(5)
                empty_projs(1, (0, 1))
                weights_high(5)
                empty_projs(1, (2, 3))
                weights_high(6)
                empty_values(6, 7)
                copy_scores(1)
                empty_projs(2, [0])
                exps(1)
                empty_projs(2, [1])
                weights_high(7)
                empty_projs(2, (2, 3))
                empty_pv(0)
                place_high(1)
                copy_scores(2)
                empty_projs(3, [0])
                exps(2)
                empty_projs(3, (1, 2, 3))
                empty_pv(1)
                place_high(2)
                copy_scores(3)
                exps(3)
                empty_pv(2)
                place_high(3)
                empty_pv(3)

            def empty(use, dst, func, bias=0.0, scale=1.0):
                act.wait_ge(full[bank_of(use)], count_of(use))
                nc.scalar.activation(dst, bank[bank_of(use)][:], func, bias=bias, scale=scale
                                     ).then_inc(free[bank_of(use)], 1)

            def mlp_high(t):
                w, high_part, _ = mlp_arrays(t)
                act.wait_ge(mlp_scaled, t + 1)
                nc.scalar.activation(high_part, w, ACT.Copy).then_inc(mlp_high_ready, 1)

            for t in range(4):
                mlp_high(t)
            log_table()
            for h in range(NH):
                squares(NH + h)
            for h in range(NH):
                logs(NH + h)
                own.wait()
                roots(NH + h)
            for t in range(4, 8):
                mlp_high(t)
            x1_high(NH)
            for h in range(NH):
                for m in range(MB):
                    n = h * MB + m
                    if n == 2:
                        x1_high(NH + 1)
                    if n >= 2:
                        act.wait_ge(hid_low_ready, n - 1)
                    use = USE_F1[h] + m
                    empty(use, gelu_of[n % 2], ACT.Gelu, bias=v_("ffn_b1", m), scale=1.0 / WSCALE)
                    act.wait_ge(free[bank_of(use)], count_of(use) + 1)
                    nc.scalar.activation(hid_pair[:, m, 0, h * HALF:(h + 1) * HALF], gelu_of[n % 2], ACT.Copy
                                         ).then_inc(hid_high_ready, 1)
            for t in range(8, 12):
                mlp_high(t)
            act.wait_ge(coup_ready, 1)

            def drive_bias(n):
                h, ob = n // KB, n % KB
                nb = B // NH
                act.wait_ge(z_used, n + 1)
                nc.scalar.activation(dbias[:, :, ob * B + h * nb:ob * B + (h + 1) * nb],
                                     drive[:, ob, h * HALF:(h + 1) * HALF].rearrange("p (b t) -> p t b", t=T),
                                     ACT.Identity, bias=v_("c2_b", ob)).then_inc(dbias_ready, 1)

            n = 0
            for h in range(NH):
                for ob in range(KB):
                    use = USE_GRU[h] + 2 * ob
                    if n >= 2:
                        act.wait_ge(z_used, n - 1)
                    empty(use, tz_of[n % 2], ACT.Tanh, bias=hb[:, ob:ob + 1], scale=0.5)
                    empty(use + 1, nn_of[n % 2], ACT.Identity, bias=v_("bn", ob))
                    if n:
                        drive_bias(n - 1)
                    act.wait_ge(gate_in, n + 1)
                    nc.scalar.activation(tn[:], nneg, ACT.Tanh, scale=0.5).then_inc(tn_ready, 1)
                    n += 1
            drive_bias(n - 1)

            with act.Fori(0, T // UNROLL) as i:
                for u, s in ((u, s) for u in range(UNROLL) for s in range(4)):
                    act.wait_ge(q_ready, i * (4 * UNROLL) + 4 * u + s + 1)
                    src = qp[:, s, 0:KB * B] if s else qn[:]
                    nc.scalar.activation(th16[:], src, ACT.Tanh).then_inc(th16_ready, 1)
                    nc.scalar.activation(th32[:], src, ACT.Tanh).then_inc(th32_ready, 1)
                    if s == 1:
                        nc.scalar.activation(
                            padded[:, :, bass.ds(i * UNROLL + u + UNROLL - 1, 1), :].rearrange("p k a b -> p (k a) b"),
                            qp[:, 0, 0:KB * B].rearrange("p (k b) -> p k b", k=KB), ACT.Copy).then_inc(trace_done, 1)
                    if (u, s) == (0, 3):
                        nc.scalar.activation(q_group.rearrange("p k (t b) -> p k t b", b=B),
                                             padded[:, :, bass.ds(i * UNROLL, UNROLL), :], ACT.Copy)
                    if 4 * u + s == LOGITS_AT:
                        nc.scalar.activation(lg[:, bass.ds(i, 1), 0:NBLK].rearrange("p a c -> p (a c)"),
                                             score[:, 1, 0:NBLK], ACT.Copy)
                    if 4 * u + s in GELU_AT:
                        half = GELU_AT.index(4 * u + s)
                        nc.scalar.activation(
                            hid_of[:, bass.ds(i, 1), half * 4:(half + 1) * 4].rearrange("p a m n -> p (a m n)"),
                            bank[half][:], ACT.Gelu)

            def last_gelu(half):
                act.wait_ge(hidden_ready, half + 1)
                nc.scalar.activation(hid_of[:, 0, half * 4:(half + 1) * 4].rearrange("p m n -> p (m n)"), bank[half][:],
                                     ACT.Gelu).then_inc(gelu_ready, 1)

            act.wait_ge(chosen, 1)
            for g in ACT_EXPANDS:
                nc.scalar.activation(*mask_of(g), ACT.Copy).then_inc(act_mask_ready, 1)
            last_gelu(0)
            for h, (places, groups) in enumerate(LAST):
                for m in range(MB):
                    n = h * MB + m
                    act.wait_ge(masked, n + 1)
                    nc.scalar.activation(masked_pair[:, places, m, 0], gelu_of[n % 2].rearrange("p (g n) -> p g n", n=P),
                                         ACT.Copy).then_inc(masked_high_ready, 1)
                    if n == 2:
                        last_gelu(1)
                    if n in ACT_EXPANDS_LATE:
                        nc.scalar.activation(*mask_of(ACT_EXPANDS_LATE[n]), ACT.Copy).then_inc(act_mask_ready, 1)

        @block.tensor
        def _(pe):
            def mm(dst, lhsT, rhs, start, stop, **kw):
                return nc.tensor.matmul(dst, lhsT, rhs, start=start, stop=stop, **kw)

            def parts3(dst, a, b):
                return sum3(dst, ((a, b),))

            def sum3(dst, operands, start=True, stop=True):
                for n, (a, b) in enumerate(operands):
                    mm(dst, a[:, 0], b[:, 0], start and n == 0, False)
                    mm(dst, a[:, 0], b[:, 1], False, False)
                    last = mm(dst, a[:, 1], b[:, 0], False, stop and n == len(operands) - 1)
                return last

            def mean_of(src, n):
                h = n % NH
                for k in range(KB):
                    last = mm(score[:, h], ones[:], src[:, k, h * HALF:(h + 1) * HALF], k == 0, k == KB - 1)
                last.then_inc(mean_ready, 1)

            def var_of(n):
                for k in range(KB):
                    pe.wait_ge(square_ready, n * KB + k + 1)
                    last = mm(var_bank(n), ones[:], square_of[n % NH][k], k == 0, k == KB - 1)
                last.then_inc(var_ready, 1)

            pe.wait_ge(ones_ready, 1)
            for h in range(NH):
                pe.wait_ge(x_loaded[h], 16)
                mean_of(x_sb, h)
            for h in range(NH):
                var_of(h)
            pe.wait_ge(small_loaded, 48)
            for c in range(6 * KB):
                for k in range(KB):
                    last = mm(bank[0][:, c * B:(c + 1) * B], adaw_sb[:, k, c * P:(c + 1) * P], cond_sb[:, k],
                              k == 0, k == KB - 1)
            last.then_inc(ada_summed, 1)
            pe.wait_ge(x1_ready, NH)

            with pe.Fori(0, NQUAD) as i:
                def fill(use):
                    pe.wait_ge(free[bank_of(use)], i * NPAR + count_of(use))
                    return bank[bank_of(use)]

                def taken(use):
                    pe.wait_ge(free[bank_of(use)], i * NPAR + count_of(use) + 1)

                def project(j):
                    pe.wait_ge(split_ready, i * NSPLIT + SPLIT_ORDER.index(("qk", j)) + 1)
                    weights = wqk_pair[:, j % 2].rearrange("p c (k w d) -> p c k w d", k=KB, w=2)
                    for h in range(NH):
                        for w in range(2):
                            use = USE_PROJ[j] + h * 2 + w
                            dst = fill(use)
                            sum3(dst[:], [(weights[:, :, k, w], x1_pair[:, :, k, h * HALF:(h + 1) * HALF])
                                          for k in range(KB)]).then_inc(full[bank_of(use)], 1)

                def scores(j):
                    taken(USE_PROJ[j] + 2)
                    taken(USE_PROJ[j] + 3)
                    if j:
                        pe.wait_ge(scores_copied, i * (QUAD * NB4) + NB4 * j)
                    for g in range(G):
                        q, k = (qk_sb[:, j % 2, w, :, g * P:(g + 1) * P] for w in range(2))
                        last = parts3(score[:, g // 4, (g % 4) * P:(g % 4 + 1) * P], q, k)
                    last.then_inc(scores_ready, 1)

                def values(*gs):
                    if gs[0] == 0:
                        pe.wait_ge(split_ready, i * NSPLIT + SPLIT_ORDER.index(("v", 1)) + 1)
                    for g in gs:
                        use = USE_V[g]
                        dst = fill(use)
                        sum3(dst[:], [(x1_pair[:, :, k, g * P:(g + 1) * P], wv_pair[:, :, k]) for k in range(KB)]
                             ).then_inc(full[bank_of(use)], 1)

                def mix(j):
                    if j == 0:
                        for g in range(G - NBANK, G):
                            taken(USE_V[g])
                    pe.wait_ge(ptx_ready, i * (QUAD * NB4) + NB4 * (j + 1))
                    for h in range(NH):
                        use = USE_PV[j] + h
                        dst = fill(use)
                        for g in range(4 * h, 4 * h + 4):
                            last = parts3(dst[:, (g % 4) * P:(g % 4 + 1) * P], v_sb[:, g, :, j * DH:(j + 1) * DH],
                                          ptx[:, :, g])
                        last.then_inc(full[bank_of(use)], 1)

                def out_project(pair, c, js):
                    use = USE_OUT[pair][c]
                    h, ob = c // KB, c % KB
                    first, end = js[0] == 2 * pair, js[-1] == 2 * pair + 1
                    if c == 0:
                        for j in js:
                            taken(USE_PV[j])
                            taken(USE_PV[j] + 1)
                        if (pair, first) == (0, True):
                            pe.wait_ge(split_ready, i * NSPLIT + SPLIT_ORDER.index(("o", 1)) + 1)
                    dst = fill(use) if first else bank[bank_of(use)]
                    last = sum3(dst[:], [(wo_pair[:, :, j, ob * P:(ob + 1) * P], ao_pair[:, j, :, h * HALF:(h + 1) * HALF])
                                         for j in js], first, end)
                    if end:
                        last.then_inc(full[bank_of(use)], 1)

                project(0)
                values(0, 1)
                scores(0)
                values(2, 3, 4, 5)
                project(1)
                values(6, 7)
                scores(1)
                project(2)
                mix(0)
                scores(2)
                project(3)
                mix(1)
                scores(3)
                out_project(0, 0, [0, 1])
                out_project(0, 1, [0, 1])
                mix(2)
                out_project(0, 2, [0, 1])
                out_project(1, 0, [2])
                out_project(1, 1, [2])
                mix(3)
                out_project(0, 3, [0, 1])
                out_project(1, 0, [3])
                out_project(1, 1, [3])
                out_project(1, 2, [2, 3])
                out_project(1, 3, [2, 3])

            def fill(use):
                pe.wait_ge(free[bank_of(use)], count_of(use))
                return bank[bank_of(use)]

            def product(use, weights, rhs, nk):
                dst = fill(use)
                for k in range(nk):
                    last = mm(dst[:], weights(k), rhs(k), k == 0, k == nk - 1)
                last.then_inc(full[bank_of(use)], 1)

            for h in range(NH):
                pe.wait_ge(x2_ready, KB * (h + 1))
                mean_of(acc, NH + h)
            for h in range(NH):
                var_of(NH + h)
            pe.wait_ge(late_loaded, 9 * 16)
            def hidden_layer(h):
                pe.wait_ge(x1_ready, NH + h + 1)
                if h == 0:
                    pe.wait_ge(mlp_split, 4)
                weights = f1_pair.rearrange("p c (k n) -> p c k n", k=KB)
                for m in range(MB):
                    dst = fill(USE_F1[h] + m)
                    sum3(dst[:], [(weights[:, :, k, m * P:(m + 1) * P], x1_pair[:, :, k, h * HALF:(h + 1) * HALF])
                                  for k in range(KB)]).then_inc(full[bank_of(USE_F1[h] + m)], 1)

            def output_layer(h):
                if h == 0:
                    pe.wait_ge(mlp_split, 8)
                dst = [fill(USE_F2[h] + ob) for ob in range(KB)]
                for m in range(MB):
                    pe.wait_ge(hid_low_ready, h * MB + m + 1)
                    for ob in range(KB):
                        s = slice(m * D + ob * P, m * D + (ob + 1) * P)
                        hi, lo = (hid_pair[:, m, c, h * HALF:(h + 1) * HALF] for c in range(2))
                        mm(dst[ob][:], f2_parts[0][:, s], hi, m == 0, False)
                        mm(dst[ob][:], f2_parts[0][:, s], lo, False, False)
                        last = mm(dst[ob][:], f2_parts[1][:, s], hi, False, m == MB - 1)
                        if m == MB - 1:
                            last.then_inc(full[bank_of(USE_F2[h] + ob)], 1)

            def gates(h):
                pe.wait_ge(x3_ready, (h + 1) * KB)
                for ob in range(KB):
                    for w, weights in enumerate((wz_sb, wn_sb)):
                        product(USE_GRU[h] + 2 * ob + w, lambda k: weights[:, k, ob * P:(ob + 1) * P],
                                lambda k: acc[:, k, h * HALF:(h + 1) * HALF], KB)

            hidden_layer(0)
            output_layer(0)
            hidden_layer(1)
            gates(0)
            output_layer(1)
            gates(1)

            def hidden(m, q):
                for k in range(KB):
                    last = mm(bank[m // 4][:, m % 4 * P:(m % 4 + 1) * P], w1_sb[:, k, m * P:(m + 1) * P], q[:, k],
                              k == 0, k == KB - 1)
                return last

            def logits(q):
                for k in range(KB):
                    last = mm(score[:, 1, 0:NBLK], q[:, k], wr_sb[:, k], k == 0, k == KB - 1)
                return last

            with pe.Fori(0, T // UNROLL) as i:
                for n in range(4 * UNROLL):
                    dst = score[:, 0]
                    pe.wait_ge(th16_ready, i * (4 * UNROLL) + n + 1)
                    first = True
                    for parts, src, ready in ((coup_parts, th16, None), (coup_parts[0:1], thlo, lo_ready)):
                        if ready is not None:
                            pe.wait_ge(ready, i * (4 * UNROLL) + n + 1)
                        for part in parts:
                            for ob in range(KB):
                                for k in range(KB):
                                    last = mm(dst[:, ob * B:(ob + 1) * B], part[:, k, ob * P:(ob + 1) * P],
                                              src[:, k * B:(k + 1) * B], first, False, skip_group_check=True)
                                    first = False
                    last.then_inc(coupled, 1)
                    m = n - FIRST_HIDDEN
                    if 0 <= m < MB:
                        hidden(m, q_group)
                    if m == MB:
                        logits(q_group)

            flat = trace.rearrange("p k t b -> p k (t b)")[:, :, B:]
            pe.wait_ge(trace_done, T + 1)
            logits(flat[:, :, N - P:]).then_inc(logits_ready, 1)

            def last_hidden(half):
                for m in range(4 * half, 4 * half + 4):
                    last = hidden(m, flat[:, :, N - P:])
                last.then_inc(hidden_ready, 1)

            last_hidden(0)
            def masks(h, m):
                n = h * MB + m
                places, groups = LAST[h]
                if n == 0:
                    pe.wait_ge(mask_ready, len(DVE_EXPANDS))
                if m == 0:
                    pe.wait_ge(act_mask_ready, len(ACT_EXPANDS) + h * len(ACT_EXPANDS_LATE))
                if n >= 3:
                    pe.wait_ge(masked, n - 2)
                for g in range(len(groups)):
                    last = mm(mask_bank(n)[:, g * P:(g + 1) * P], maskx[:, places.start + g, m * P:(m + 1) * P],
                              ident[:], True, True)
                last.then_inc(maskb_ready, 1)

            for m in range(3):
                masks(0, m)
            last_hidden(1)
            for h, (places, groups) in enumerate(LAST):
                dst = [fill(USE_G2[h] + ob) for ob in range(KB)]
                for k in range(MB):
                    pe.wait_ge(h_ready, h * MB + k + 1)
                    for ob in range(KB):
                        s = slice(k * D + ob * P, k * D + (ob + 1) * P)
                        hi, lo = (masked_pair[:, places, k, c] for c in range(2))
                        mm(dst[ob][:], w2_pair[:, 0, s], hi, k == 0, False)
                        mm(dst[ob][:], w2_pair[:, 0, s], lo, False, False)
                        last = mm(dst[ob][:], w2_pair[:, 1, s], hi, False, k == MB - 1)
                        if k == MB - 1:
                            last.then_inc(full[bank_of(USE_G2[h] + ob)], 1)
                    n = h * MB + k + 3
                    if n < NH * MB:
                        masks(n // MB, n % MB)

        @block.vector
        def _(dve):
            own = Own(dve, dve_step)
            V = nc.vector
            for b in range(NBANK):
                V.memset(sq[:, b:b + 1], 0.0).then_inc(free[b], 1)
            V.memset(eps[:], LN_EPS).then_inc(eps_ready, 1)
            own.step(V.memset(lg[:, :, NBLK:], BIG))

            def mod(c, k, h):
                nb = HALF // T
                return ada[:, c, k, h * nb:(h + 1) * nb].unsqueeze(2).broadcast_to([P, nb, T])

            def tok(ap):
                return ap.rearrange("p (b t) -> p b t", t=T)

            def centre(src, n):
                h = n % NH
                dve.wait_ge(mean_ready, n + 1)
                for k in range(KB):
                    V.tensor_tensor(centred_of[h][k], src[:, k, h * HALF:(h + 1) * HALF], score[:, h], ALU.subtract
                                    ).then_inc(centred_ready, 1)

            def normalised(n, dst):
                h = n % NH
                s = slice(h * HALF, (h + 1) * HALF)
                dve.wait_ge(rstd_ready, n + 1)
                own.step(V.tensor_tensor(newton, rstd[:, h], rstd[:, h], ALU.mult))
                own.wait()
                own.step(V.scalar_tensor_tensor(newton, newton, -0.5, var[:, h], ALU.mult, ALU.mult))
                own.wait()
                own.step(V.scalar_tensor_tensor(rstd[:, h], newton, 1.5, rstd[:, h], ALU.add, ALU.mult))
                own.wait()
                for k in range(KB):
                    own.step(V.tensor_tensor(dst[:, k, s], centred_of[h][k], rstd[:, h], ALU.mult))

            def modulate(n, shift, scale, dst, apart=False):
                h = n % NH
                s = slice(h * HALF, (h + 1) * HALF)
                own.wait()
                for k in range(KB):
                    own.step(V.tensor_tensor(tok(dst[:, k, s]), tok(dst[:, k, s]), mod(scale, k, h), ALU.mult))
                own.wait()
                for k in range(KB):
                    last = V.tensor_tensor(tok(dst[:, k, s]), tok(dst[:, k, s]), mod(shift, k, h), ALU.add)
                    if apart:
                        last.then_inc(normed, 1)
                    elif k < KB - 1:
                        own.step(last)
                if apart:
                    for k in range(KB):
                        dve.wait_ge(x1_high_ready, n * KB + k + 1)
                        last = V.tensor_tensor(x1_pair[:, 1, k, s], dst[:, k, s], x1_pair[:, 0, k, s], ALU.subtract)
                        if k < KB - 1:
                            own.step(last)
                last.then_inc(x1_ready, 1)

            for h in range(NH):
                dve.wait_ge(x_loaded[h], 16)
                centre(x_sb, h)
            dve.wait_ge(small_loaded, 48)
            for k in range(KB):
                own.step(V.tensor_copy(acc[:, k], v_("out_b", k).broadcast_to([P, N])))
            for h in range(NH):
                normalised(h, drive)
            dve.wait_ge(ada_summed, 1)
            own.step(V.tensor_tensor(
                ada[:].rearrange("p a k b -> p (a k) b"), bank[0][:, 0:12 * B].rearrange("p (a b) -> p a b", b=B),
                v_("ada_b").unsqueeze(2).broadcast_to([P, 12, B]), ALU.add))
            own.wait()
            for c in (SCALE1, SCALE2):
                own.step(V.tensor_scalar(ada[:, c], ada[:, c], 1.0, None, ALU.add))
            for h in range(NH):
                modulate(h, SHIFT1, SCALE1, drive, True)
            own.wait()

            STEPS = QUAD * 4
            PAIRS = 4 * QUAD + G + NH * QUAD
            start = own.n
            with dve.Fori(0, NQUAD) as i:
                own.n, own.base = 0, i * STEPS + start
                for w, name in enumerate(("q_b", "k_b", "v_b")):
                    V.tensor_scalar(pass_b[:, w], vec[:, bass.ds(i * QUAD + VEC[name][0], QUAD)], WSCALE, None,
                                    ALU.mult).then_inc(bias_ready, 1)
                dve.wait_ge(bias_ready, i * 3 + 3)
                pairs = [0]

                def low(use, hi, lo, bias=None):
                    pairs[0] += 1
                    dve.wait_ge(high_ready, i * PAIRS + pairs[0])
                    if bias is None:
                        ins = V.tensor_tensor(lo, bank[bank_of(use)][:], hi, ALU.subtract)
                    else:
                        ins = V.scalar_tensor_tensor(lo, bank[bank_of(use)][:], bias, hi, ALU.add, ALU.subtract)
                    ins.then_inc(free[bank_of(use)], 1)

                def low_proj(j, k):
                    h, w = k // 2, k % 2
                    hi, lo = (qk_sb[:, j % 2, w, c, h * HALF:(h + 1) * HALF] for c in range(2))
                    low(USE_PROJ[j] + k, hi, lo, pass_b[:, w, j:j + 1])

                def shift(j):
                    dve.wait_ge(scores_copied, i * (QUAD * NB4) + NB4 * (j + 1))
                    own.step(V.tensor_reduce(smax[:], sraw[:], AX_X, ALU.max))
                    own.wait()
                    V.tensor_tensor(sc[:], sraw[:], smax[:].unsqueeze(2).broadcast_to([P, G, T]), ALU.subtract
                                    ).then_inc(shifted, 1)

                def normalise(j):
                    dve.wait_ge(exp_ready, i * QUAD + j + 1)
                    own.step(V.tensor_reduce(ssum[:], pe_[:], AX_X, ALU.add))
                    own.wait()
                    own.step(V.reciprocal(srec[:], ssum[:]))
                    own.wait()
                    own.step(V.tensor_tensor(pn[:], pe_[:], srec[:].unsqueeze(2).broadcast_to([P, G, T]), ALU.mult))
                    own.wait()
                    if j:
                        dve.wait_ge(ptx_ready, i * (QUAD * NB4) + NB4 * j)
                    V.transpose(pt[:].rearrange("p g t -> p (g t)"), pn[:].rearrange("p g t -> p (g t)")
                                ).then_inc(pt_ready, 1)

                def low_projs(j):
                    for k in range(4):
                        low_proj(j, k)

                def low_values(*gs):
                    for g in gs:
                        low(USE_V[g], v_sb[:, g, 0], v_sb[:, g, 1])

                def low_pv(j):
                    for h in range(NH):
                        hi, lo = (ao_pair[:, j, c, h * HALF:(h + 1) * HALF] for c in range(2))
                        low(USE_PV[j] + h, hi, lo, pass_b[:, 2, j:j + 1])

                def add_heads(pair, c):
                    use = USE_OUT[pair][c]
                    a = acc[:, c % KB, c // KB * HALF:(c // KB + 1) * HALF]
                    dve.wait_ge(full[bank_of(use)], i * NPAR + count_of(use))
                    V.scalar_tensor_tensor(a, bank[bank_of(use)][:], WSCALE ** -2, a, ALU.mult, ALU.add
                                           ).then_inc(free[bank_of(use)], 1)

                low_projs(0)
                low_values(0, 1)
                shift(0)
                low_values(2)
                normalise(0)
                low_values(3, 4, 5)
                low_projs(1)
                low_values(6, 7)
                shift(1)
                normalise(1)
                low_projs(2)
                low_pv(0)
                shift(2)
                normalise(2)
                low_projs(3)
                low_pv(1)
                shift(3)
                add_heads(0, 0)
                normalise(3)
                add_heads(0, 1)
                low_pv(2)
                add_heads(0, 2)
                low_pv(3)
                add_heads(0, 3)
                for c in range(KB * NH):
                    add_heads(1, c)
                assert own.n == STEPS and pairs[0] == PAIRS
            own.n, own.base = start + NQUAD * STEPS, 0
            for use in range(AFTER - NBANK, AFTER):
                dve.wait_ge(free[bank_of(use)], count_of(use) + 1)

            for h in range(NH):
                s = slice(h * HALF, (h + 1) * HALF)
                for ob in range(KB):
                    own.step(V.tensor_tensor(tok(acc[:, ob, s]), tok(acc[:, ob, s]), mod(GATE1, ob, h), ALU.mult))
                own.wait()
                for ob in range(KB):
                    V.tensor_tensor(acc[:, ob, s], acc[:, ob, s], x_sb[:, ob, s], ALU.add).then_inc(x2_ready, 1)
            dve.wait_ge(x2_ready, KB * NH)
            for h in range(NH):
                centre(acc, NH + h)
            for h in range(NH):
                normalised(NH + h, drive)
                modulate(NH + h, SHIFT2, SCALE2, drive, True)

            def hidden_lows(h):
                for m in range(MB):
                    n = h * MB + m
                    hi, lo = (hid_pair[:, m, c, h * HALF:(h + 1) * HALF] for c in range(2))
                    dve.wait_ge(hid_high_ready, n + 1)
                    V.tensor_tensor(lo, gelu_of[n % 2], hi, ALU.subtract).then_inc(hid_low_ready, 1)

            def wait_full(use):
                dve.wait_ge(full[bank_of(use)], count_of(use))

            def residual(h):
                s = slice(h * HALF, (h + 1) * HALF)
                for ob in range(KB):
                    use = USE_F2[h] + ob
                    wait_full(use)
                    tmp = centred[:, ob]
                    V.scalar_tensor_tensor(tok(tmp), tok(bank[bank_of(use)][:]), 1.0 / WSCALE, mod(GATE2, ob, h),
                                           ALU.mult, ALU.mult).then_inc(free[bank_of(use)], 1)
                    dve.wait_ge(free[bank_of(use)], count_of(use) + 1)
                    V.tensor_tensor(acc[:, ob, s], acc[:, ob, s], tmp, ALU.add).then_inc(x3_ready, 1)

            def min_gru(h):
                s = slice(h * HALF, (h + 1) * HALF)
                for ob in range(KB):
                    n = h * KB + ob
                    use = USE_GRU[h] + 2 * ob

                    def coefficients():
                        dve.wait_ge(free[bank_of(use)], count_of(use) + 1)
                        own.step(V.tensor_scalar(za[:], tz_of[n % 2], -0.5, 0.5, ALU.mult, ALU.add))
                        own.step(V.tensor_scalar(zb, tz_of[n % 2], 0.5, 0.5, ALU.mult, ALU.add))

                    if ob == 0:
                        coefficients()
                    dve.wait_ge(free[bank_of(use + 1)], count_of(use + 1) + 1)
                    V.tensor_scalar(nneg, nn_of[n % 2], 0.0, None, ALU.min).then_inc(gate_in, 1)
                    if ob:
                        coefficients()
                    own.step(V.tensor_scalar(npos[:], nn_of[n % 2], 0.0, 0.5, ALU.max, ALU.add))
                    dve.wait_ge(tn_ready, n + 1)
                    own.wait()
                    own.step(V.scalar_tensor_tensor(npos[:], tn[:], 0.5, npos[:], ALU.mult, ALU.add))
                    own.wait()
                    own.step(V.tensor_tensor(zb, zb, npos[:], ALU.mult))
                    own.wait()
                    a0, b0 = tok(za[:])[:, :, 0:1], tok(zb)[:, :, 0:1]
                    own.step(V.scalar_tensor_tensor(b0, a0, 0.5, b0, ALU.mult, ALU.add))
                    own.wait()
                    own.step(V.memset(a0, 0.0))
                    own.wait()
                    own.step(V.tensor_tensor_scan(npos[:], za[:], zb, 0.0, ALU.mult, ALU.add))
                    own.wait()
                    V.tensor_tensor(drive[:, ob, s], x_sb[:, ob, s], npos[:], ALU.add).then_inc(z_used, 1)
                    dve.wait_ge(z_used, n + 1)

            own.step(V.memset(padded[:, :, 0:UNROLL - 1], 0.0))
            V.tensor_copy(qp[:, 0, KB * B:], cond_sb[:].rearrange("p k b -> p (k b)")).then_inc(p_ready, 1)
            own.wait()
            hidden_lows(0)
            dve.wait_ge(late_loaded, 9 * 16)
            own.step(V.tensor_scalar(coup_rest[:], coup_sb[:], CSCALE, None, ALU.mult))
            own.wait()
            own.step(V.tensor_copy(coup_parts[0][:], coup_rest[:]))
            own.wait()
            own.step(V.tensor_tensor(coup_parts[1][:], coup_rest[:], coup_parts[0][:], ALU.subtract))
            own.wait()
            V.tensor_scalar(hb[:], v_("bz"), 0.5, None, ALU.mult).then_inc(coup_ready, 1)

            bias2 = sq[:].rearrange("p (k b) -> p k b", k=KB)
            own.step(V.tensor_tensor(bias2, ada[:, GATE2], v_("ffn_b2").unsqueeze(2).broadcast_to([P, KB, B]), ALU.mult))
            own.wait()
            for k in range(KB):
                own.step(V.tensor_tensor(tok(acc[:, k]), tok(acc[:, k]),
                                         bias2[:, k].unsqueeze(2).broadcast_to([P, B, T]), ALU.add))
            own.wait()
            residual(0)
            hidden_lows(1)
            dve.wait_ge(hid_low_ready, NH * MB)
            min_gru(0)
            residual(1)
            min_gru(1)
            V.tensor_copy(qn[:], cond_sb[:].rearrange("p k b -> p (k b)")).then_inc(q_ready, 1)
            dve.wait_ge(p_ready, 1)
            dve.wait_ge(q_ready, 1)
            dve.wait_ge(dbias_ready, KB * NH)

            H1, H2, H6 = STAGE_H[0], STAGE_H[2], STAGE_H[3]
            RK = 23
            start = own.n
            stt = V.scalar_tensor_tensor
            w64 = KB * B
            q_, p_ = (lambda s: qp[:, s, 0:w64]), (lambda s: qp[:, s, w64:])
            with dve.Fori(0, T // UNROLL) as i:
                own.n, own.base = 0, i * (UNROLL * RK) + start

                def mark(ins):
                    own.step(ins)
                    return own.n

                def wait_for(n):
                    dve.wait_ge(dve_step, own.base + n)

                for u in range(UNROLL):
                    t4, t3 = i * (4 * UNROLL) + 4 * u, i * (3 * UNROLL) + 3 * u
                    d_t = dbias[:, bass.ds(i * UNROLL + u, 1)].rearrange("p a c -> p (a c)")
                    V.tensor_scalar(q_(0), qn[:], CLAMP, -CLAMP, ALU.min, ALU.max).then_inc(clip_ready, 1)
                    dve.wait_ge(clip_ready, i * UNROLL + u + 1)
                    for s in range(4):
                        hs = STAGE_H[s]
                        if s == 1:
                            lined = mark(stt(lin[:, 1], p_(1), -H1, qd[:, 0], ALU.mult, ALU.add))
                        if s == 2:
                            wait_for(behind)
                            lined = mark(stt(lin[:, 0], p_(2), -H2, qd[:, 1], ALU.mult, ALU.add))
                        if s == 3:
                            wait_for(behind)
                            lined4 = mark(stt(lin4[:], comb[:], 1.0 / 3.0, d6[:], ALU.mult, ALU.add))
                        if s:
                            dve.wait_ge(q_ready, t4 + s + 1)
                        if s == 0:
                            lined = mark(stt(qd[:, 0], d_t, H1, q_(0), ALU.mult, ALU.add))
                        squared = mark(V.tensor_tensor(sq[:], q_(s), q_(s), ALU.mult))
                        if s == 0:
                            wait_for(lined)
                            lined = mark(stt(lin[:, 0], p_(0), -H1, qd[:, 0], ALU.mult, ALU.add))
                        if s in (1, 2):
                            dve.wait_ge(bp_ready, t3 + s + 1)
                            stt(p_(s + 1), q_(s), hs * EPSILON, bp[:], ALU.mult, ALU.add).then_inc(p_ready, 1)
                        if s == 3:
                            wait_for(lined4)
                            lined = mark(stt(lin[:, 1], p_(3), -H6, lin4[:], ALU.mult, ALU.add))
                            dve.wait_ge(pacc_ready, i * UNROLL + u + 1)
                            pended = mark(stt(pend[:], q_(3), H6 * EPSILON, pacc[:], ALU.mult, ALU.add))
                        dve.wait_ge(th32_ready, t4 + s + 1)
                        V.tensor_tensor(thlo[:], th32[:], th16[:], ALU.subtract).then_inc(lo_ready, 1)
                        wait_for(squared)
                        cubed = mark(stt(cub[:], sq[:], -3.0 if s < 3 else -3.0 - 1.0 / hs, q_(s), ALU.add, ALU.mult))
                        if s == 0:
                            dve.wait_ge(bp_ready, t3 + 1)
                            stt(p_(1), q_(0), hs * EPSILON, bp[:], ALU.mult, ALU.add).then_inc(p_ready, 1)
                        if s == 1:
                            differed = mark(V.tensor_tensor(comb[:], q_(1), q_(0), ALU.subtract))
                        if s == 2:
                            wait_for(differed)
                            mark(stt(comb[:], q_(2), 2.0, comb[:], ALU.mult, ALU.add))
                        if s == 3:
                            wait_for(pended)
                            V.tensor_scalar(p_(0), pend[:], CLAMP, -CLAMP, ALU.min, ALU.max).then_inc(p_ready, 1)
                        wait_for(cubed)
                        based = mark(stt(base[:], cub[:], -hs / 3.0, lin[:, s % 2], ALU.mult, ALU.add))
                        if s == 1:
                            behind = mark(stt(qd[:, 1], d_t, H2, q_(0), ALU.mult, ALU.add))
                        if s == 2:
                            behind = mark(V.tensor_scalar(d6[:], d_t, H6, None, ALU.mult))
                        dve.wait_ge(p_ready, t4 + s + 2)
                        wait_for(based)
                        dve.wait_ge(coupled, t4 + s + 1)
                        stt(q_(s + 1) if s < 3 else qn[:], score[:, 0, 0:w64], hs / CSCALE, base[:], ALU.mult, ALU.add
                            ).then_inc(q_ready, 1)
                    dve.wait_ge(q_ready, t4 + 5)
                assert own.n == RK * UNROLL, own.n
            own.n, own.base = start + T * RK, 0
            V.tensor_scalar(trace[:, :, T], qn[:].rearrange("p (k b) -> p k b", k=KB), CLAMP, -CLAMP, ALU.min,
                            ALU.max).then_inc(trace_done, 1)

            dve.wait_ge(logits_ready, 1)
            own.step(V.tensor_copy(lg[:, 0, 0:NBLK], score[:, 1, 0:NBLK]))
            own.wait()
            own.step(V.tensor_tensor(lg[:, :, 0:NBLK], lg[:, :, 0:NBLK],
                                     br_sb[:].unsqueeze(1).broadcast_to([P, G, NBLK]), ALU.add))
            own.wait()
            for g in range(G):
                own.step(V.max(top8[:, g], lg[:, g]))
            own.wait()
            for g in range(G):
                own.step(V.match_replace(lgr[:, g], top8[:, g], lg[:, g], -BIG))
            own.wait()
            V.tensor_scalar(mask[:], lgr[:, :, 0:NBLK], -BIG, None, ALU.is_equal).then_inc(chosen, 1)
            dve.wait_ge(chosen, 1)
            for g in DVE_EXPANDS:
                V.tensor_copy(*mask_of(g)).then_inc(mask_ready, 1)
            for h, (places, groups) in enumerate(LAST):
                if G - 1 in groups:
                    dve.wait_ge(gelu_ready, 2)

                def low_part(m):
                    n = h * MB + m
                    dve.wait_ge(masked_high_ready, n + 1)
                    V.tensor_tensor(masked_pair[:, places, m, 1], gelu_of[n % 2].rearrange("p (g n) -> p g n", n=P),
                                    masked_pair[:, places, m, 0], ALU.subtract).then_inc(h_ready, 1)

                for m in range(MB):
                    n = h * MB + m
                    dve.wait_ge(maskb_ready, n + 1)
                    if n >= 2:
                        dve.wait_ge(h_ready, n - 1)
                    V.tensor_tensor(gelu_of[n % 2].rearrange("p (g n) -> p g n", n=P), hid_of[:, places, m],
                                    mask_bank(n).rearrange("p (g n) -> p g n", n=P), ALU.mult).then_inc(masked, 1)
                    if m:
                        low_part(m - 1)
                low_part(MB - 1)
            for h, (places, groups) in enumerate(LAST):
                for ob in range(KB):
                    use = USE_G2[h] + ob
                    wait_full(use)
                    at = 0
                    for a, b in runs(groups):
                        V.scalar_tensor_tensor(osb[:, ob, a * P:b * P].rearrange("p (t b) -> p t b", b=B),
                                        bank[bank_of(use)][:, at * P:(at + b - a) * P].rearrange(
                                            "p (t b) -> p t b", b=B), 1.0 / WSCALE,
                                        drive[:, ob].rearrange("p (b t) -> p t b", t=T)[:, a * UNROLL:b * UNROLL],
                                        ALU.mult, ALU.add).then_inc(out_ready, 1)
                        at += b - a


def kernel(**inputs):
    import numpy as np
    import concourse.bacc as bacc
    from concourse.bass_utils import run_bass_kernel_spmd

    a = {k: np.asarray(v) for k, v in inputs.items()}

    def rows(w, *shape):
        return w.reshape(-1, P, *w.shape[1:]).swapaxes(0, 1).reshape(P, -1, *(shape or w.shape[1:]))

    def column(v):
        return v.reshape(-1, P).T

    qkv = a["L0_cond_qkv_w"].reshape(KB, P, 3, H, DH)
    arrays = {
        "xT": rows(a["x"].transpose(2, 0, 1).reshape(D, N)),
        "condT": rows(a["cond_2048"].T),
        "ada_w": rows(a["L0_cond_ada_w"]),
        "vecs": np.concatenate([column(v) for v in (
            a["L0_cond_ada_b"], *a["L0_cond_qkv_b"].reshape(3, -1), a["L0_cond_out_b"], a["L0_cond_ffn_b1"],
            a["L0_cond_ffn_b2"], a["L0_attn_bz"], a["L0_attn_bn"], a["L0_cond2_bias"])], axis=1),
        "br": np.repeat(a["L0_ffn_br"][None], P, axis=0),
        "wqk": qkv[:, :, 0:2].transpose(3, 1, 0, 2, 4),
        "wv": qkv[:, :, 2].reshape(KB, P, NQUAD, QUAD * DH).transpose(2, 1, 0, 3),
        "wo": a["L0_cond_out_w"].reshape(H, DH, D).transpose(1, 0, 2),
        "ffn_w1": rows(a["L0_cond_ffn_w1"]),
        "ffn_w2": rows(a["L0_cond_ffn_w2"]),
        "wzT": rows(a["L0_attn_Wz"].T),
        "wnT": rows(a["L0_attn_Wn"].T),
        "coupT": rows(a["L0_cond2_coupling"].T),
        "wrT": rows(a["L0_ffn_Wr"].T),
        "w1T": rows(a["L0_ffn_W1"].T),
        "w2T": rows(a["L0_ffn_W2"].T),
    }
    arrays = {k: np.ascontiguousarray(v) for k, v in arrays.items()}
    nc = bacc.Bacc("TRN2", target_bir_lowering=False, num_devices=1)
    args = [nc.dram_tensor(k, v.shape, mybir.dt.from_np(v.dtype), kind="ExternalInput").ap() for k, v in arrays.items()]
    out = nc.dram_tensor("out_0_dram", (P, KB, N), F32, kind="ExternalOutput").ap()
    build(nc, *args, out)
    r = run_bass_kernel_spmd(nc, [arrays], core_ids=[0])
    got = r.results[0]["out_0_dram"].reshape(P, KB, T, B)
    return np.ascontiguousarray(got.transpose(3, 2, 1, 0).reshape(B, T, D))
```
